# Optimizing a Trainium2 kernel written in Bass

```python
import numpy as np
import jax
import jax.numpy as jnp

def _softmax(x, axis=-1):
    return jax.nn.softmax(x, axis=axis)

def _gelu(x):
    return jax.nn.gelu(x, approximate=True)

def _silu(x):
    return jax.nn.silu(x)

def _sigmoid(x):
    return jax.nn.sigmoid(x)

def _layernorm(x, axis=-1, eps=1e-05):
    m = jnp.mean(x, axis=axis, keepdims=True)
    v = jnp.var(x, axis=axis, keepdims=True)
    return (x - m) / jnp.sqrt(v + eps)

def _scatter_add(tgt, idx, src, axis=0):
    return tgt.at[idx].add(src)

def _segment_sum(src, seg, n):
    return jax.ops.segment_sum(src, seg, n)
kernel_name = 'mk_xattn_seq_d2_seqx_r4_5400b1'

def setup_inputs(seed: int=0):
    np.random.seed(seed)
    _w = jnp.asarray

    def _rec_inputs():
        import jax
        import jax.numpy as jnp
        _rk = jax.random.key(seed)
        x = -0.000929 + 1 * jax.random.normal(jax.random.fold_in(_rk, 1), (16, 512, 256), jnp.float32)
        _lenS = 512 - jax.random.randint(jax.random.fold_in(_rk, 7), (16,), 0, max(1, 512 // 4) + 1, jnp.int32)
        _lenS2 = 64 - jax.random.randint(jax.random.fold_in(_rk, 8), (16,), 0, max(1, 64 // 4) + 1, jnp.int32)
        _ctx_768P = jax.random.normal(jax.random.fold_in(_rk, 11), (16, 16, 192), jnp.float32)
        _ctx_768c = jax.random.dirichlet(jax.random.fold_in(_rk, 511), 0.3 * jnp.ones((16,), jnp.float32), (16, 64))
        _ctx_768t = jnp.einsum('bsk,bkd->bsd', _ctx_768c, _ctx_768P)
        _ctx_768t = _ctx_768t * jax.lax.rsqrt(jnp.mean(jnp.square(_ctx_768t)) + 1e-12) * 0.953939
        ctx_768 = -0.00286756 + 0.998052 * (_ctx_768t + 0.3 * jax.random.normal(jax.random.fold_in(_rk, 611), (16, 64, 192), jnp.float32))
        return (x, ctx_768)
    x, ctx_768 = _rec_inputs()

    def _L0_xattn_setup():
        import jax, jax.numpy as jnp
        import numpy as np
        B_, S_, P_, D_ = (2, 128, 64, 256)
        L_ = 4
        DI_ = 2 * D_
        DS_ = 16
        DC_ = 4
        DR_ = D_ // 16
        PCD_ = 192

        def rmsnorm(x, w, eps=1e-05):
            return x * jax.lax.rsqrt(jnp.mean(x * x, axis=-1, keepdims=True) + eps) * w

        def mamba_block(x, ip_w, cw, cb, xp_w, dtp_w, dtp_b, A_log, Dp, op_w):
            B, S, _ = x.shape
            xz = jnp.einsum('bsd,ed->bse', x, ip_w)
            xi, z = jnp.split(xz, 2, axis=-1)
            xt = xi.transpose(0, 2, 1)
            conv = jax.lax.conv_general_dilated(xt, cw[:, None, :], (1,), [(DC_ - 1, 0)], feature_group_count=DI_) + cb[:, None]
            xi = jax.nn.silu(conv.transpose(0, 2, 1))
            xdbl = jnp.einsum('bse,fe->bsf', xi, xp_w)
            dt, Bm, Cm = jnp.split(xdbl, [DR_, DR_ + DS_], axis=-1)
            dt = jax.nn.softplus(jnp.einsum('bsr,er->bse', dt, dtp_w) + dtp_b)
            A = -jnp.exp(A_log)
            dA = jnp.exp(dt[..., None] * A)
            dBu = dt[..., None] * Bm[:, :, None, :] * xi[..., None]

            def step(h, t):
                da, dbu, c = t
                h = da * h + dbu
                return (h, jnp.einsum('bes,bs->be', h, c))
            h0 = jnp.zeros((B, DI_, DS_), x.dtype)
            _, ys = jax.lax.scan(step, h0, (dA.transpose(1, 0, 2, 3), dBu.transpose(1, 0, 2, 3), Cm.transpose(1, 0, 2)))
            y = ys.transpose(1, 0, 2) + xi * Dp
            y = y * jax.nn.silu(z)
            return jnp.einsum('bse,de->bsd', y, op_w)
        key = jax.random.key(seed)
        ks = jax.random.split(key, 12)
        n = lambda k, s, sc=0.02: jax.random.normal(k, s, dtype=jnp.float32) * sc
        A_log = jnp.log(jnp.broadcast_to(jnp.arange(1, DS_ + 1, dtype=jnp.float32), (L_, DI_, DS_)))
        return {'x': jax.random.normal(ks[0], (B_, S_, D_), dtype=jnp.float32), 'prepend_cond': jax.random.normal(ks[1], (B_, P_, PCD_), dtype=jnp.float32), 'pre_w1': n(ks[2], (PCD_, D_)), 'pre_w2': n(ks[3], (D_, D_)), 'norm_w': jnp.ones((L_, D_), jnp.float32), 'in_proj_w': n(ks[4], (L_, 2 * DI_, D_)), 'conv_w': n(ks[5], (L_, DI_, DC_), 0.1), 'conv_b': jnp.zeros((L_, DI_), jnp.float32), 'x_proj_w': n(ks[6], (L_, DR_ + 2 * DS_, DI_)), 'dt_proj_w': n(ks[7], (L_, DI_, DR_), 0.1), 'dt_proj_b': jax.random.uniform(ks[8], (L_, DI_), jnp.float32, -4.0, -2.0), 'A_log': A_log, 'D_param': jnp.ones((L_, DI_), jnp.float32), 'out_proj_w': n(ks[9], (L_, D_, DI_)), 'final_norm_w': jnp.ones((D_,), jnp.float32)}
    _L0_xattn_all = _L0_xattn_setup()
    _L0_xattn_in = {k: v for k, v in _L0_xattn_all.items() if k in ('pre_w1', 'pre_w2', 'norm_w', 'in_proj_w', 'conv_w', 'conv_b', 'x_proj_w', 'dt_proj_w', 'dt_proj_b', 'A_log', 'D_param', 'out_proj_w', 'final_norm_w')}
    del _L0_xattn_all

    def _L1_xattn_setup():
        import jax, jax.numpy as jnp
        import numpy as np
        DIM1, DIM2, H = (256, 192, 16)
        HID = 4 * DIM1
        EPS = 1e-05

        def layernorm(x, w, b):
            mu = jnp.mean(x, axis=-1, keepdims=True)
            var = jnp.mean((x - mu) ** 2, axis=-1, keepdims=True)
            return (x - mu) * jax.lax.rsqrt(var + EPS) * w + b
        key = jax.random.key(seed)
        ks = jax.random.split(key, 12)
        s1 = 1.0 / np.sqrt(DIM1)
        s2 = 1.0 / np.sqrt(DIM2)
        sh = 1.0 / np.sqrt(HID)
        return {'x': jax.random.normal(ks[0], (4, 256, DIM1), jnp.float32), 'y': jax.random.normal(ks[1], (4, 256, DIM2), jnp.float32), 'ln1_w': jnp.ones((DIM1,), jnp.float32), 'ln1_b': jnp.zeros((DIM1,), jnp.float32), 'ln2_w': jnp.ones((DIM2,), jnp.float32), 'ln2_b': jnp.zeros((DIM2,), jnp.float32), 'ln3_w': jnp.ones((DIM1,), jnp.float32), 'ln3_b': jnp.zeros((DIM1,), jnp.float32), 'Wq': jax.random.uniform(ks[2], (DIM1, DIM1), jnp.float32, -s1, s1), 'Wkv': jax.random.uniform(ks[3], (DIM2, 2 * DIM1), jnp.float32, -s2, s2), 'Wproj': jax.random.uniform(ks[4], (DIM1, DIM1), jnp.float32, -s1, s1), 'bproj': jnp.zeros((DIM1,), jnp.float32), 'W1': jax.random.uniform(ks[5], (DIM1, HID), jnp.float32, -s1, s1), 'b1': jnp.zeros((HID,), jnp.float32), 'W2': jax.random.uniform(ks[6], (HID, DIM1), jnp.float32, -sh, sh), 'b2': jnp.zeros((DIM1,), jnp.float32)}
    _L1_xattn_all = _L1_xattn_setup()
    _L1_xattn_in = {k: v for k, v in _L1_xattn_all.items() if k in ('ln1_w', 'ln1_b', 'ln2_w', 'ln2_b', 'ln3_w', 'ln3_b', 'Wq', 'Wkv', 'Wproj', 'bproj', 'W1', 'b1', 'W2', 'b2')}
    del _L1_xattn_all
    return {'x': x, 'ctx_768': ctx_768, 'L0_xattn_pre_w1': _L0_xattn_in['pre_w1'], 'L0_xattn_pre_w2': _L0_xattn_in['pre_w2'], 'L0_xattn_norm_w': _L0_xattn_in['norm_w'], 'L0_xattn_in_proj_w': _L0_xattn_in['in_proj_w'], 'L0_xattn_conv_w': _L0_xattn_in['conv_w'], 'L0_xattn_conv_b': _L0_xattn_in['conv_b'], 'L0_xattn_x_proj_w': _L0_xattn_in['x_proj_w'], 'L0_xattn_dt_proj_w': _L0_xattn_in['dt_proj_w'], 'L0_xattn_dt_proj_b': _L0_xattn_in['dt_proj_b'], 'L0_xattn_A_log': _L0_xattn_in['A_log'], 'L0_xattn_D_param': _L0_xattn_in['D_param'], 'L0_xattn_out_proj_w': _L0_xattn_in['out_proj_w'], 'L0_xattn_final_norm_w': _L0_xattn_in['final_norm_w'], 'L1_xattn_ln1_w': _L1_xattn_in['ln1_w'], 'L1_xattn_ln1_b': _L1_xattn_in['ln1_b'], 'L1_xattn_ln2_w': _L1_xattn_in['ln2_w'], 'L1_xattn_ln2_b': _L1_xattn_in['ln2_b'], 'L1_xattn_ln3_w': _L1_xattn_in['ln3_w'], 'L1_xattn_ln3_b': _L1_xattn_in['ln3_b'], 'L1_xattn_Wq': _L1_xattn_in['Wq'], 'L1_xattn_Wkv': _L1_xattn_in['Wkv'], 'L1_xattn_Wproj': _L1_xattn_in['Wproj'], 'L1_xattn_bproj': _L1_xattn_in['bproj'], 'L1_xattn_W1': _L1_xattn_in['W1'], 'L1_xattn_b1': _L1_xattn_in['b1'], 'L1_xattn_W2': _L1_xattn_in['W2'], 'L1_xattn_b2': _L1_xattn_in['b2']}

def reference(x, ctx_768, L0_xattn_pre_w1, L0_xattn_pre_w2, L0_xattn_norm_w, L0_xattn_in_proj_w, L0_xattn_conv_w, L0_xattn_conv_b, L0_xattn_x_proj_w, L0_xattn_dt_proj_w, L0_xattn_dt_proj_b, L0_xattn_A_log, L0_xattn_D_param, L0_xattn_out_proj_w, L0_xattn_final_norm_w, L1_xattn_ln1_w, L1_xattn_ln1_b, L1_xattn_ln2_w, L1_xattn_ln2_b, L1_xattn_ln3_w, L1_xattn_ln3_b, L1_xattn_Wq, L1_xattn_Wkv, L1_xattn_Wproj, L1_xattn_bproj, L1_xattn_W1, L1_xattn_b1, L1_xattn_W2, L1_xattn_b2):
    import jax
    import jax.numpy as jnp

    def _L0_xattn_ref(x, prepend_cond, pre_w1, pre_w2, norm_w, in_proj_w, conv_w, conv_b, x_proj_w, dt_proj_w, dt_proj_b, A_log, D_param, out_proj_w, final_norm_w):
        import jax, jax.numpy as jnp
        import numpy as np
        B_, S_, P_, D_ = (2, 128, 64, 256)
        L_ = 4
        DI_ = 2 * D_
        DS_ = 16
        DC_ = 4
        DR_ = D_ // 16
        PCD_ = 192

        def rmsnorm(x, w, eps=1e-05):
            return x * jax.lax.rsqrt(jnp.mean(x * x, axis=-1, keepdims=True) + eps) * w

        def mamba_block(x, ip_w, cw, cb, xp_w, dtp_w, dtp_b, A_log, Dp, op_w):
            B, S, _ = x.shape
            xz = jnp.einsum('bsd,ed->bse', x, ip_w)
            xi, z = jnp.split(xz, 2, axis=-1)
            xt = xi.transpose(0, 2, 1)
            conv = jax.lax.conv_general_dilated(xt, cw[:, None, :], (1,), [(DC_ - 1, 0)], feature_group_count=DI_) + cb[:, None]
            xi = jax.nn.silu(conv.transpose(0, 2, 1))
            xdbl = jnp.einsum('bse,fe->bsf', xi, xp_w)
            dt, Bm, Cm = jnp.split(xdbl, [DR_, DR_ + DS_], axis=-1)
            dt = jax.nn.softplus(jnp.einsum('bsr,er->bse', dt, dtp_w) + dtp_b)
            A = -jnp.exp(A_log)
            dA = jnp.exp(dt[..., None] * A)
            dBu = dt[..., None] * Bm[:, :, None, :] * xi[..., None]

            def step(h, t):
                da, dbu, c = t
                h = da * h + dbu
                return (h, jnp.einsum('bes,bs->be', h, c))
            h0 = jnp.zeros((B, DI_, DS_), x.dtype)
            _, ys = jax.lax.scan(step, h0, (dA.transpose(1, 0, 2, 3), dBu.transpose(1, 0, 2, 3), Cm.transpose(1, 0, 2)))
            y = ys.transpose(1, 0, 2) + xi * Dp
            y = y * jax.nn.silu(z)
            return jnp.einsum('bse,de->bsd', y, op_w)
        p = jax.nn.silu(prepend_cond @ pre_w1) @ pre_w2
        h = jnp.concatenate([p, x], axis=1)
        for l in range(L_):
            h = h + mamba_block(rmsnorm(h, norm_w[l]), in_proj_w[l], conv_w[l], conv_b[l], x_proj_w[l], dt_proj_w[l], dt_proj_b[l], A_log[l], D_param[l], out_proj_w[l])
        h = rmsnorm(h, final_norm_w)
        return h[:, P_:, :]

    def _L1_xattn_ref(x, y, ln1_w, ln1_b, ln2_w, ln2_b, ln3_w, ln3_b, Wq, Wkv, Wproj, bproj, W1, b1, W2, b2):
        import jax, jax.numpy as jnp
        import numpy as np
        DIM1, DIM2, H = (256, 192, 16)
        HID = 4 * DIM1
        EPS = 1e-05

        def layernorm(x, w, b):
            mu = jnp.mean(x, axis=-1, keepdims=True)
            var = jnp.mean((x - mu) ** 2, axis=-1, keepdims=True)
            return (x - mu) * jax.lax.rsqrt(var + EPS) * w + b
        B, N1, C1 = x.shape
        hd = C1 // H
        scale = hd ** (-0.5)
        xn = layernorm(x, ln1_w, ln1_b)
        yn = layernorm(y, ln2_w, ln2_b)
        q = (xn @ Wq).reshape(B, N1, H, hd).transpose(0, 2, 1, 3)
        kv = (yn @ Wkv).reshape(B, y.shape[1], 2, H, hd)
        k = kv[:, :, 0].transpose(0, 2, 1, 3)
        v = kv[:, :, 1].transpose(0, 2, 1, 3)
        attn = jax.nn.softmax(jnp.einsum('bhqd,bhkd->bhqk', q, k) * scale, axis=-1)
        o = jnp.einsum('bhqk,bhkd->bhqd', attn, v).transpose(0, 2, 1, 3).reshape(B, N1, C1)
        x = x + (o @ Wproj + bproj)
        h = jax.nn.gelu(layernorm(x, ln3_w, ln3_b) @ W1 + b1, approximate=False)
        x = x + (h @ W2 + b2)
        return x
    x = _L0_xattn_ref(x, ctx_768, L0_xattn_pre_w1, L0_xattn_pre_w2, L0_xattn_norm_w, L0_xattn_in_proj_w, L0_xattn_conv_w, L0_xattn_conv_b, L0_xattn_x_proj_w, L0_xattn_dt_proj_w, L0_xattn_dt_proj_b, L0_xattn_A_log, L0_xattn_D_param, L0_xattn_out_proj_w, L0_xattn_final_norm_w)
    x = _L1_xattn_ref(x, ctx_768, L1_xattn_ln1_w, L1_xattn_ln1_b, L1_xattn_ln2_w, L1_xattn_ln2_b, L1_xattn_ln3_w, L1_xattn_ln3_b, L1_xattn_Wq, L1_xattn_Wkv, L1_xattn_Wproj, L1_xattn_bproj, L1_xattn_W1, L1_xattn_b1, L1_xattn_W2, L1_xattn_b2)
    return x

_drawn_inputs = setup_inputs


def setup_inputs(seed=0):
    import zlib

    import numpy as np

    out = dict(_drawn_inputs(seed))
    spreads = {'L0_xattn_norm_w': (1.0, 0.6),
     'L0_xattn_conv_b': (0.0, 0.8),
     'L0_xattn_D_param': (1.0, 0.6),
     'L0_xattn_final_norm_w': (1.0, 0.2),
     'L1_xattn_ln1_w': (1.0, 0.6),
     'L1_xattn_ln1_b': (0.0, 2.0),
     'L1_xattn_ln2_w': (1.0, 0.2),
     'L1_xattn_ln2_b': (0.0, 0.278),
     'L1_xattn_ln3_w': (1.0, 0.2),
     'L1_xattn_ln3_b': (0.0, 0.414),
     'L1_xattn_bproj': (0.0, 0.1),
     'L1_xattn_b1': (0.0, 0.1),
     'L1_xattn_b2': (0.0, 0.1)}
    factors = {'L0_xattn_pre_w1': 8.0,
     'L0_xattn_pre_w2': 8.0,
     'L0_xattn_in_proj_w': 5.81,
     'L0_xattn_conv_w': 8.0,
     'L0_xattn_x_proj_w': 8.0,
     'L0_xattn_dt_proj_w': 8.0,
     'L0_xattn_dt_proj_b': 8.0,
     'L0_xattn_A_log': 8.0,
     'L0_xattn_out_proj_w': 5.768}
    for name, (base, spread) in spreads.items():
        noise = np.random.default_rng([zlib.crc32(name.encode()), seed]).standard_normal(out[name].shape)
        drawn = base * np.exp(spread * noise) if base else spread * noise
        out[name] = jnp.asarray(drawn.astype(out[name].dtype))
    for name, factor in factors.items():
        out[name] = (out[name] * factor).astype(out[name].dtype)
    return out
```

```python
import concourse.bass as bass
from concourse import mybir
from contextlib import ExitStack

F32 = mybir.dt.float32
BF16 = mybir.dt.bfloat16
ALU = mybir.AluOpType
ACT = mybir.ActivationFunctionType
AX = mybir.AxisListType

P = 128
B, S, D = 16, 512, 256
LC, DC = 64, 192
L, DI, DS, TAPS, DR = 4, 512, 16, 4, 16
T = LC + S
TH = T // 2
KD = D // P
KI = DI // P
SLOTS = 4
BLOCKS = B // SLOTS
STEPS = L * SLOTS
CH = P // DS
G = DI // CH
GC = G // KI
QUAD = 4
RING = 4
PRING = 8
XP = DR + 2 * DS
HEADS, HD = 16, 16
HID = 4 * D
EPS = 1e-5
NP = KD + KI * TAPS + KI + KI
IN_RANGE = "a loop's count masked to the range"

PREP_PAIRS = ["ms", "xi0", "xi1", "xi2", "xi3", "xp", "dt0", "dt1", "B", "C", "dt2", "dt3"]
AT = {"ms": (1, 2), "xi0": (6, 7), "out0": (8, 10), "xi1": (11, 12), "out1": (13, 15), "xi2": (16, 17),
      "z0": (18, 19), "xi3": (20, 21), "z1": (24, 25), "xp": (28, 30), "dt0": (32, 33), "dt1": (34, 35),
      "B": (37, 38), "C": (39, 40), "z2": (42, 44), "dt2": (46, 47), "dt3": (48, 49), "z3": (52, 54)}
BODY_PAIRS = list(AT)
VECTOR_PREP = (["square", "norm0", "norm1"]
               + [f"{s}{c}" for c in range(KI) for s in ("tap0_", "tap1_", "tap2_", "silu")]
               + ["low0", "rest0", "guard0", "dtx0", "low1", "rest1", "guard1", "dtx1"])
SCALAR_PREP = (["rstd", "tanh0", "tanh1", "tanh2", "tanh3"]
               + [f"{s}{h}" for h in range(2) for s in ("exp", "ln", "hi_d", "hi_x", "mid_d", "mid_x")])
POOL_PREP = [f"{s}{h}" for h in range(2) for s in ("log", "dt", "r_d", "r_x", "lo_d", "lo_x")]
GATED = [f"{s}{c}" for c in range(KI) for s in ("skip", "gate")]


class Steps:

    def __init__(self, sem, names, credit=None):
        self.sem, self.names, self.per = sem, names, len(names)
        self.credit = self.per if credit is None else credit

    def upto(self, n, name):
        return self.before(n, self.names.index(name) + 1)

    def before(self, n, k=0):
        return n * self.per + (self.credit + k)


def program(nc, xT, ctxT, w_early, ip_x, ip_z, xp_w, dt_w, op_w, a_log, d_par, pre_w1, pre_w2, cst, avec,
            wq, wk, wv, wp, w1, w2, b2, out):
    ctx = ExitStack()
    with ctx:
        def sb(name, shape, dt=F32):
            return ctx.enter_context(nc.sbuf_tensor(name, shape, dt))

        def pb(name, shape):
            return ctx.enter_context(nc.psum_tensor(name, shape, F32))

        def sem(name):
            return ctx.enter_context(nc.semaphore(name))

        hT = sb("hT", [P, SLOTS, KD, T])
        csts = sb("csts", [P, 1448])
        spread = sb("spread", [P, QUAD, P], BF16)
        sum_states = csts[:, 512:640].rearrange("p (j m) -> p j m", j=QUAD)
        sel_B = csts[:, 640:768]
        sel_C = csts[:, 768:896]
        ident = csts[:, 896:1024]
        head_mask = csts[:, 1024:1032]
        v_mask = csts[:, 1032:1064]
        ones_x = csts[:, 1064:1192]
        ones_c = csts[:, 1192:1320]
        one_row = csts[0:1, 1320:1448]
        avecs = sb("avecs", [P, 32])
        ln1_w, ln1_b, ln3_w, ln3_b, bproj, fin_w = (avecs[:, 2 * i:2 * i + 2] for i in range(6))
        b1_v, ln2_w, ln2_b = avecs[:, 12:20], avecs[:, 20:22], avecs[:, 22:24]
        negA = sb("negA", [P, L, G])
        Dall = sb("Dall", [P, L, KI])
        curA = sb("curA", [P, G])
        curD = sb("curD", [P, KI])
        ARENA = 46480
        arena = sb("arena", [P, ARENA])
        at = [0]

        def view(*shape, dt=F32):
            n = 1
            for s in shape:
                n *= s
            words = n if dt == F32 else n // 2
            assert at[0] + words <= ARENA, at[0] + words
            v = arena[:, at[0]:at[0] + words]
            at[0] += words
            if dt != F32:
                v = v.bitcast(dt)
            if len(shape) == 2:
                v = v.rearrange("p (a b) -> p a b", a=shape[0])
            if len(shape) == 3:
                v = v.rearrange("p (a b c) -> p a b c", a=shape[0], b=shape[1])
            return v

        dA = view(RING, T)
        ring = view(PRING, T)
        st = {"d": view(2, 8, T, dt=BF16), "x": view(2, 8, T, dt=BF16)}
        xn = view(KD, T)
        xnz = view(KD, T)
        square_low = view(KD, T)
        rstd = view(T)
        xpad = view(2, T + TAPS - 1 + 1)
        acc = view(2, T)
        th = view(2, T)
        xs = view(KI, T)
        xsD = view(KI, T)
        xdbl = view(T)
        Bst, Cst, Brep, Crep = view(T), view(T), view(T), view(T)
        rl, u, lg, dt = view(2, T), view(2, T), view(2, T), view(2, T)
        part = {k: view(2, T, dt=BF16) for k in ("hi_d", "mid_d", "lo_d", "hi_x", "mid_x", "lo_x")}
        thz = view(2, TH)
        yt = view(T)
        yg = view(KI, T)
        ipx = view(KD, DI)
        ipz = view(KD, DI)
        xpw = view(KI, XP)
        dtw = view(DI)
        opw = view(KI, D)
        lv = view(NP + 2)
        norm_w = lv[:, 0:KD]
        taps = lv[:, KD:KD + KI * TAPS].rearrange("p (c k) -> p c k", c=KI)
        conv_b = lv[:, KD + KI * TAPS:KD + KI * TAPS + KI]
        dt_b = lv[:, KD + KI * TAPS + KI:NP]
        assert at[0] <= ARENA
        at[0] = 0
        sq = view(SLOTS, KD, S)
        xna = view(SLOTS, KD, S)
        q = view(SLOTS, KD, S)
        rs = view(SLOTS, S)
        oT = sq
        ctxs = view(KD, SLOTS * LC)
        cc = view(KD, SLOTS * LC)
        csq = view(KD, SLOTS * LC)
        crs = view(SLOTS * LC)
        cn2 = view(KD, SLOTS, 2 * LC)
        kT = view(KD, SLOTS * LC)
        Kbd = view(SLOTS * KD, 8, LC)
        Vbd = view(SLOTS, 8, 32)
        prob = view(2, 4, 8 * LC)
        mx = view(2, 8)
        den = view(2, 8)
        rden = view(2, 8)
        pT = view(4, S)
        hid = view(2, 8, S)
        otile = view(2, D)
        wq_s, wk_s, wv_s, wp_s = view(KD, D), view(KD, D), view(KD, D), view(KD, D)
        w1_s = view(KD, HID)
        w2_s = view(8, D)
        b2_s = view(D)
        preh = view(KD, SLOTS * LC)
        pw1, pw2 = wq_s, wk_s

        bank = [pb(f"bank{i}", [P, 2, 512]) for i in range(4)]
        dt_ps, dtx_ps, y_ps, job_ps = bank

        cst_loaded, cst_ready = sem("cst_loaded"), sem("cst_ready")
        cst_exp, cst_neg, pad_ready = sem("cst_exp"), sem("cst_neg"), sem("pad_ready")
        h_loaded, ctx_loaded, aw_loaded = sem("h_loaded"), sem("ctx_loaded"), sem("aw_loaded")
        early_loaded, z_loaded, o_loaded = sem("early_loaded"), sem("z_loaded"), sem("o_loaded")
        early_ready, zw_ready, ow_ready = sem("early_ready"), sem("zw_ready"), sem("ow_ready")
        zw_free, ow_free = sem("zw_free"), sem("ow_free")
        stacked = {(k, h): sem(f"stacked_{k}{h}") for k in "dx" for h in range(2)}
        job_done = sem("job_done")
        job_read = [sem("job_read0"), sem("job_read1")]
        dt_rep = Steps(sem("dt_spread"), range(G))
        dtx_rep = Steps(sem("dtx_spread"), range(G))
        decay = Steps(sem("decay_ready"), range(G))
        inp = Steps(sem("input_ready"), range(G))
        state = Steps(sem("state_ready"), range(G))
        prod = Steps(sem("product_ready"), range(G // 2))
        summed = Steps(sem("states_summed"), range(G // QUAD))
        gated = Steps(sem("gated"), GATED)
        cur = Steps(sem("cur_ready"), ["B", "A", "D"])
        cur_C = Steps(sem("cur_C_ready"), ["C"])
        skip_x = Steps(sem("skip_ready"), range(KI))
        z_in = Steps(sem("z_input_ready"), ["xnz"])
        z_tanh = Steps(sem("z_tanh"), range(2 * KI))
        vprep = Steps(sem("vector_prep"), VECTOR_PREP)
        sprep = Steps(sem("scalar_prep"), SCALAR_PREP)
        pprep = Steps(sem("pool_prep"), POOL_PREP)
        block_scanned = sem("block_scanned")
        steps = [dt_rep, dtx_rep, decay, inp, state, prod, summed, gated, cur, cur_C, skip_x, z_in, z_tanh,
                 vprep, sprep, pprep]

        jobs = [("pre1", 0), ("pre1", 1), ("pre2", 0), ("pre2", 1)]
        jobs += [("ms", b) for b in range(SLOTS)] + [("cmean",)]
        jobs += [("mean", b) for b in range(SLOTS)] + [("cvar",)]
        jobs += [("var", b) for b in range(SLOTS)]
        jobs += [("k", m) for m in range(KD)] + [("v", b) for b in range(SLOTS)]
        jobs += [("q", b, m) for b in range(SLOTS) for m in range(KD)]
        units = [(b, m) for b in range(SLOTS) for m in range(KD)]
        for i, (b, m) in enumerate(units):
            jobs += [("score", b, m, r) for r in range(4)]
            if i:
                pbm = units[i - 1]
                jobs += [("turn", *pbm, r) for r in range(4)] + [("pv", *pbm)]
        jobs += [("turn", *units[-1], r) for r in range(4)] + [("pv", *units[-1])]
        jobs += [("proj", b, m) for b in range(SLOTS) for m in range(KD)]
        jobs += [("mean3", b) for b in range(SLOTS)] + [("var3", b) for b in range(SLOTS)]
        for b in range(SLOTS):
            jobs += [("up", b, f) for f in range(8)]
            if b:
                jobs += [("down", b - 1, r) for r in range(4)]
        jobs += [("down", SLOTS - 1, r) for r in range(4)]
        number = {j: i for i, j in enumerate(jobs)}
        on_bank = [len(range(k, len(jobs), 8)) for k in range(8)]
        adone = sem("attention_job_done")
        aread = [sem(f"attention_job_read{i}") for i in range(8)]

        def abank(j):
            i = number[j] % 8
            return bank[i // 2][:, i % 2, :]

        def await_job(eng, bk, j):
            eng.wait_ge(adone, bk * len(jobs) + (number[j] + 1))

        def read_sem(j):
            return aread[number[j] % 8]

        def await_read(eng, bk, j):
            eng.wait_ge(read_sem(j), bk * on_bank[number[j] % 8] + (number[j] // 8 + 2))

        def await_bank(eng, bk, j):
            eng.wait_ge(read_sem(j), bk * on_bank[number[j] % 8] + (number[j] // 8 + 1))

        def await_reads(eng, bk, j, read):
            count = {number[j] % 8: number[j] // 8}
            for i in (number[x] for x in read):
                count[i % 8] = max(count.get(i % 8, 0), i // 8 + 1)
            for k, c in count.items():
                eng.wait_ge(aread[k], bk * on_bank[k] + (c + 1))

        R4 = range(SLOTS)
        tiles = [(b, m, r) for b, m in units for r in range(4)]
        av = Steps(sem("attention_vector"),
                   [f"sq{b}" for b in R4] + [f"fin{b}{k}" for b in R4 for k in range(KD)]
                   + ["ccen0", "csq0", "csq1"] + [f"{s}{b}" for b in R4 for s in ("cen", "csq_")]
                   + ["cn0", "cn1"] + [f"xn{b}{k}" for b in R4 for k in range(KD)]
                   + [f"kbd{b}{m}" for b, m in units]
                   + [f"{s}{i - (s != 'max')}" for i in range(33) for s in ("max", "sum", "rec")
                      if (i < 32 if s == "max" else i > 0)]
                   + [f"{s}{b}" for b in R4 for s in ("den", "dsq")]
                   + [f"yn{b}{k}" for b in R4 for k in range(KD)], 1)
        asc = Steps(sem("attention_scalar"),
                    [f"rs{b}" for b in R4] + ["crs"] + [f"rv{b}" for b in R4] + ["cb0", "cb1", "cb0d", "cb1d"]
                    + [f"xb{b}{k}" for b in R4 for k in range(KD)] + [f"e{i}" for i in range(32)]
                    + [f"r3{b}" for b in R4] + [f"yb{b}{k}" for b in R4 for k in range(KD)], 1)
        apl = Steps(sem("attention_pool"), [f"p{i}" for i in range(32)], 1)
        stored = [sem("stored0"), sem("stored1")]
        head_loaded = sem("head_loaded")

        def pair_index(order, base, name):
            return base + order.index(name)

        FIRST = [p for p in BODY_PAIRS if p[:3] != "out"]
        LAST = [p for p in BODY_PAIRS if p not in PREP_PAIRS]
        OUTS = ["out0", "out1"]

        def walk(eng, prepare_first, body, finish, attend, head):
            with eng.Fori(0, BLOCKS) as bk:
                head(bk)
                n0, b0 = bk * STEPS, bk * (18 * STEPS)
                prepare_first(b0, n0)
                body(FIRST, b0 + 12, n0)
                with eng.Fori(1, STEPS - 1) as it:
                    body(BODY_PAIRS, b0 + it * 18 + 10, n0 + it)
                nl = n0 + (STEPS - 1)
                body(LAST, b0 + (18 * (STEPS - 1) + 10), nl)
                finish(b0 + (18 * STEPS - 2), nl)
                attend(bk)

        block = ctx.enter_context(nc.Block())

        @block.tensor
        def _(pe):
            def spread_dt(n, g):
                c, j, qq = g // GC, (g % GC) // QUAD, g % QUAD
                if g % (G // 2) == 0:
                    pe.wait_ge(stacked["d", g // (G // 2)], (n + 1) * 192 + 16)
                pe.wait_ge(decay.sem, decay.before(n, g))
                for h in range(2):
                    i = nc.tensor.matmul(dt_ps[:, h, 0:TH], spread[0:96, j, :],
                                         st["d"][0:96, c // 2, (c % 2) * 4 + qq, h * TH:(h + 1) * TH],
                                         start=True, stop=True)
                i.then_inc(dt_rep.sem, 1)

            def spread_dtx(n, g):
                c, j, qq = g // GC, (g % GC) // QUAD, g % QUAD
                if g % (G // 2) == 0:
                    pe.wait_ge(stacked["x", g // (G // 2)], (n + 1) * 192 + 16)
                pe.wait_ge(inp.sem, inp.before(n, g))
                for h in range(2):
                    i = nc.tensor.matmul(dtx_ps[:, h, 0:TH], spread[0:96, j, :],
                                         st["x"][0:96, c // 2, (c % 2) * 4 + qq, h * TH:(h + 1) * TH],
                                         start=True, stop=True)
                i.then_inc(dtx_rep.sem, 1)

            def sum_quad(n, k):
                pe.wait_ge(prod.sem, prod.before(n, 2 * k + 2))
                j = k % QUAD
                if j == 0:
                    pe.wait_ge(gated.sem, gated.before(n, 2 * (k // QUAD) - 1))
                for h in range(2):
                    for qq in range(QUAD):
                        slot = (QUAD * k + qq) % PRING
                        i = nc.tensor.matmul(y_ps[32 * qq:32 * qq + 32, h, 0:TH], sum_states[:, j, :],
                                             ring[:, slot, h * TH:(h + 1) * TH],
                                             start=(j == 0), stop=(j == QUAD - 1))
                i.then_inc(summed.sem, 1)

            def job(order, base, n, m, name, h):
                k = pair_index(order, base, name)
                pe.wait_ge(job_read[h], k + 1)
                t = slice(h * TH, (h + 1) * TH)
                o = job_ps[:, h, 0:TH]
                if name == "ms":
                    pe.wait_ge(vprep.sem, vprep.upto(m, "square"))
                    for kk in range(KD):
                        i = nc.tensor.matmul(o, ones_x, square_low[:, kk, t], start=kk == 0, stop=kk == KD - 1)
                elif name[:2] == "xi":
                    c = int(name[2])
                    pe.wait_ge(early_ready, m + 1)
                    pe.wait_ge(vprep.sem, vprep.upto(m, "norm1"))
                    for kk in range(KD):
                        i = nc.tensor.matmul(o, ipx[:, kk, c * P:(c + 1) * P], xn[:, kk, t],
                                             start=kk == 0, stop=kk == KD - 1)
                elif name == "xp":
                    pe.wait_ge(vprep.sem, vprep.upto(m, "silu3"))
                    for c in range(KI):
                        i = nc.tensor.matmul(job_ps[0:XP, h, 0:TH], xpw[:, c, :], xs[:, c, t],
                                             start=c == 0, stop=c == KI - 1)
                elif name[:2] == "dt":
                    c = int(name[2])
                    kx = pair_index(order, base, "xp")
                    pe.wait_ge(job_read[h], kx + 2)
                    i = nc.tensor.matmul(o, dtw[0:DR, c * P:(c + 1) * P], xdbl[0:DR, t], start=True, stop=True)
                elif name in "BC":
                    i = nc.tensor.matmul(o, (sel_B if name == "B" else sel_C)[0:XP, :], xdbl[0:XP, t],
                                         start=True, stop=True)
                elif name[0] == "z":
                    c = int(name[1])
                    pe.wait_ge(zw_ready, n + 1)
                    pe.wait_ge(z_in.sem, z_in.upto(n, "xnz"))
                    for kk in range(KD):
                        i = nc.tensor.matmul(o, ipz[:, kk, c * P:(c + 1) * P], xnz[:, kk, t],
                                             start=kk == 0, stop=kk == KD - 1)
                else:
                    mm = int(name[3])
                    pe.wait_ge(ow_ready, n)
                    pe.wait_ge(gated.sem, gated.upto(n - 1, "gate3"))
                    for c in range(KI):
                        i = nc.tensor.matmul(o, opw[:, c, mm * P:(mm + 1) * P], yg[:, c, t],
                                             start=c == 0, stop=c == KI - 1)
                i.then_inc(job_done, 1)

            def body(order, base, n):
                last, first = "ms" not in order, "out0" not in order
                for g in range(G):
                    if g + 1 < G:
                        spread_dt(n, g + 1)
                        spread_dtx(n, g + 1)
                    elif not last:
                        spread_dt(n + 1, 0)
                        spread_dtx(n + 1, 0)
                    if g % QUAD == 2:
                        if g > 2:
                            sum_quad(n, g // QUAD - 1)
                        elif not first:
                            sum_quad(n - 1, G // QUAD - 1)
                    for name in order:
                        for h in range(2):
                            if AT[name][h] == g:
                                job(order, base, n, n + 1, name, h)

            def attention(bk):
                def product(j, parts, rows=slice(0, P), cols=512, read=()):
                    await_reads(pe, bk, j, read)
                    o = abank(j)[rows, 0:cols]
                    if len(parts[0][1].shape) == 3:
                        o = o.rearrange("p (a b) -> p a b", a=parts[0][1].shape[1])
                    for i, (lhs, rhs) in enumerate(parts):
                        last = nc.tensor.matmul(o, lhs, rhs, start=i == 0, stop=i == len(parts) - 1)
                    last.then_inc(adone, 1)

                def kp(k):
                    return slice(0, P if k == 0 else DC - P)

                X = [[hT[:, b, k, LC:T] for k in range(KD)] for b in R4]
                for b in R4:
                    pe.wait_ge(av.sem, av.upto(bk, f"sq{b}"))
                    product(("ms", b), [(ones_x, sq[:, b, k, :]) for k in range(KD)])
                pe.wait_ge(ctx_loaded, bk * 32 + 32)
                product(("cmean",), [(ones_c[kp(k), :], ctxs[kp(k), k, :]) for k in range(KD)], cols=SLOTS * LC)
                for b in R4:
                    pe.wait_ge(av.sem, av.upto(bk, f"fin{b}1"))
                    product(("mean", b), [(ones_x, X[b][k]) for k in range(KD)])
                pe.wait_ge(av.sem, av.upto(bk, "csq1"))
                product(("cvar",), [(ones_c[kp(k), :], csq[kp(k), k, :]) for k in range(KD)], cols=SLOTS * LC)
                for b in R4:
                    pe.wait_ge(av.sem, av.upto(bk, f"csq_{b}"))
                    product(("var", b), [(ones_x, sq[:, b, k, :]) for k in range(KD)])
                pe.wait_ge(aw_loaded, bk * 144 + 144)
                pe.wait_ge(asc.sem, asc.upto(bk, "cb1"))
                for m in range(KD):
                    product(("k", m), [(wk_s[kp(k), k, m * P:(m + 1) * P], cn2[kp(k), k, :, 0:LC])
                                       for k in range(KD)], cols=SLOTS * LC)
                pe.wait_ge(asc.sem, asc.upto(bk, "cb1d"))
                for b in R4:
                    product(("v", b), [(cn2[kp(k), k, b, :], wv_s[kp(k), k, :]) for k in range(KD)], cols=D)
                for b in R4:
                    pe.wait_ge(asc.sem, asc.upto(bk, f"xb{b}1"))
                    for m in range(KD):
                        product(("q", b, m), [(wq_s[:, k, m * P:(m + 1) * P], xna[:, b, k, :]) for k in range(KD)])

                def turn(b, m):
                    for r in range(4):
                        j = ("turn", b, m, r)
                        pe.wait_ge(apl.sem, apl.upto(bk, f"p{tiles.index((b, m, 3))}"))
                        await_bank(pe, bk, j)
                        for qb in range(4):
                            i = nc.tensor.matmul(abank(j)[:, qb * P:(qb + 1) * P],
                                                 prob[:, m, qb, r * P:(r + 1) * P], ident,
                                                 start=qb == 0, stop=qb == 3)
                        i.then_inc(adone, 1)
                    j = ("pv", b, m)
                    await_reads(pe, bk, j, [("v", b)] + [("turn", b, m, r) for r in range(4)])
                    for r in range(4):
                        i = nc.tensor.matmul(abank(j)[32 * r:32 * r + 32, :], Vbd[:, b, m * 4 + r, :],
                                             pT[:, r, :], start=True, stop=True)
                    i.then_inc(adone, 1)

                for i, (b, m) in enumerate(units):
                    for r in range(4):
                        pe.wait_ge(av.sem, av.upto(bk, f"kbd{b}{m}"))
                        product(("score", b, m, r),
                                [(q[:, b, m, r * P:(r + 1) * P], Kbd[:, KD * b + m, :, :])], read=[("q", b, m)])
                    if i:
                        turn(*units[i - 1])
                turn(*units[-1])
                for b in R4:
                    for m in range(KD):
                        product(("proj", b, m), [(wp_s[:, k, m * P:(m + 1) * P], oT[:, b, k, :]) for k in range(KD)],
                                read=[("pv", b, k) for k in range(KD)])
                for b in R4:
                    product(("mean3", b), [(ones_x, X[b][k]) for k in range(KD)],
                            read=[("proj", b, k) for k in range(KD)])
                for b in R4:
                    pe.wait_ge(av.sem, av.upto(bk, f"dsq{b}"))
                    product(("var3", b), [(ones_x, sq[:, b, k, :]) for k in range(KD)])

                def down(b):
                    for r in range(4):
                        j = ("down", b, r)
                        await_reads(pe, bk, j, [("up", b, f) for f in range(8)])
                        o, t = abank(j), slice(r * P, (r + 1) * P)
                        nc.tensor.matmul(o[:, 0:D], one_row, b2_s[0:1, :], start=True, stop=False)
                        for k in range(KD):
                            nc.tensor.matmul(o[:, k * P:(k + 1) * P], X[b][k][:, t], ident, start=False, stop=False)
                        for f in range(8):
                            i = nc.tensor.matmul(o[:, 0:D], hid[:, b % 2, f, t], w2_s[:, f, :],
                                                 start=False, stop=f == 7)
                        i.then_inc(adone, 1)

                for b in R4:
                    pe.wait_ge(asc.sem, asc.upto(bk, f"yb{b}1"))
                    for f in range(8):
                        product(("up", b, f), [(w1_s[:, k, f * P:(f + 1) * P], xna[:, b, k, :]) for k in range(KD)])
                    if b:
                        down(b - 1)
                down(SLOTS - 1)

            def head(bk):
                pe.wait_ge(head_loaded, bk * 80 + 80)
                for m in range(KD):
                    j = ("pre1", m)
                    await_bank(pe, bk, j)
                    for k, rows in ((0, P), (1, DC - P)):
                        i = nc.tensor.matmul(abank(j)[:, 0:SLOTS * LC], pw1[0:rows, k, m * P:(m + 1) * P],
                                             ctxs[0:rows, k, :], start=k == 0, stop=k == 1)
                    i.then_inc(adone, 1)
                for m in range(KD):
                    await_read(pe, bk, ("pre1", m))
                for m in range(KD):
                    j = ("pre2", m)
                    await_bank(pe, bk, j)
                    for k in range(KD):
                        i = nc.tensor.matmul(abank(j)[:, 0:SLOTS * LC], pw2[:, k, m * P:(m + 1) * P], preh[:, k, :],
                                             start=k == 0, stop=k == 1)
                    i.then_inc(adone, 1)

            def prepare_first(base, m):
                for name in PREP_PAIRS:
                    for h in range(2):
                        job(PREP_PAIRS, base, m, m, name, h)
                spread_dt(m, 0)
                spread_dtx(m, 0)

            def finish(base, nl):
                sum_quad(nl, G // QUAD - 1)
                for name in OUTS:
                    for h in range(2):
                        job(OUTS, base, nl + 1, nl, name, h)

            def attend(bk):
                pe.wait_ge(block_scanned, bk + 1)
                attention(bk)

            pe.wait_ge(cst_ready, 1)
            walk(pe, prepare_first, body, finish, attend, head)

        @block.scalar
        def _(act):
            def halves(v):
                return v.rearrange("p (h t) -> p h t", h=2)

            def job_ready(order, base, name, h):
                act.wait_ge(job_done, pair_index(order, base, name) * 2 + (h + 1))

            def decay_of(n, g):
                if g == 0:
                    act.wait_ge(cur.sem, cur.upto(n, "A"))
                act.wait_ge(state.sem, state.before(n, g - RING + 1))
                act.wait_ge(dt_rep.sem, dt_rep.before(n, g + 1))
                nc.scalar.activation(halves(dA[:, g % RING, :]), dt_ps[:, :, 0:TH], ACT.Exp,
                                     scale=curA[:, g:g + 1]).then_inc(decay.sem, 1)

            def root(order, base, m):
                act.wait_ge(vprep.sem, vprep.before(m))
                for h in range(2):
                    job_ready(order, base, "ms", h)
                    nc.scalar.activation(rstd[:, h * TH:(h + 1) * TH], job_ps[:, h, 0:TH], ACT.Ln,
                                         bias=EPS).then_inc(job_read[h], 1)
                k = pair_index(order, base, "ms")
                act.wait_ge(job_read[0], k + 2)
                act.wait_ge(job_read[1], k + 2)
                nc.scalar.activation(rstd, rstd, ACT.Exp, scale=-0.5).then_inc(sprep.sem, 1)

            def take_xi(order, base, m, c, h):
                if h == 0:
                    prior = vprep.upto(m, f"silu{c - 2}") if c > 1 else vprep.upto(m - 1, f"silu{c + 2}")
                    act.wait_ge(vprep.sem, prior)
                job_ready(order, base, f"xi{c}", h)
                nc.scalar.activation(xpad[:, c % 2, TAPS - 1 + h * TH:TAPS - 1 + (h + 1) * TH],
                                     job_ps[:, h, 0:TH], ACT.Copy)
                nc.scalar.activation(acc[:, c % 2, h * TH:(h + 1) * TH], job_ps[:, h, 0:TH], ACT.Identity,
                                     bias=conv_b[:, c:c + 1], scale=taps[:, c, TAPS - 1:TAPS]
                                     ).then_inc(job_read[h], 1)

            def tanh_conv(m, c):
                act.wait_ge(vprep.sem, vprep.upto(m, f"tap2_{c}"))
                nc.scalar.activation(th[:, c % 2, :], acc[:, c % 2, :], ACT.Tanh, scale=0.5
                                     ).then_inc(sprep.sem, 1)

            def take_xp(order, base, h):
                job_ready(order, base, "xp", h)
                nc.scalar.activation(xdbl[0:XP, h * TH:(h + 1) * TH], job_ps[0:XP, h, 0:TH], ACT.Copy,
                                     scale=0.5).then_inc(job_read[h], 1)

            def take_dt(order, base, m, c, h):
                if h == 0 and c % 2 == 0:
                    act.wait_ge(pprep.sem, pprep.upto(m, "dt0") if c else pprep.upto(m - 1, "dt1"))
                job_ready(order, base, f"dt{c}", h)
                t = slice(h * TH, (h + 1) * TH)
                nc.scalar.activation(u[:, c % 2, t], job_ps[:, h, 0:TH], ACT.Abs, bias=dt_b[:, c:c + 1])
                nc.scalar.activation(rl[:, c % 2, t], job_ps[:, h, 0:TH], ACT.Relu, bias=dt_b[:, c:c + 1]
                                     ).then_inc(job_read[h], 1)

            def softplus(order, base, m, hc):
                k = pair_index(order, base, f"dt{2 * hc + 1}")
                act.wait_ge(job_read[0], k + 2)
                act.wait_ge(job_read[1], k + 2)
                nc.scalar.activation(u, u, ACT.Exp, scale=-1.0).then_inc(sprep.sem, 1)
                act.wait_ge(sprep.sem, sprep.upto(m, f"exp{hc}"))
                act.wait_ge(pprep.sem, pprep.upto(m, "lo_x0") if hc else pprep.upto(m - 1, "lo_x1"))
                nc.scalar.activation(lg, u, ACT.Ln, bias=1.0).then_inc(sprep.sem, 1)

            def high(m, hc, k):
                if k == "d":
                    act.wait_ge(pprep.sem, pprep.upto(m, f"dt{hc}"))
                else:
                    act.wait_ge(vprep.sem, vprep.upto(m, f"dtx{hc}"))
                act.wait_ge(stacked[k, 1 - hc], (m + hc) * 192 + 16)
                nc.scalar.activation(part["hi_" + k], dt if k == "d" else lg, ACT.Copy).then_inc(sprep.sem, 1)

            def middle(m, hc, k):
                act.wait_ge(pprep.sem, pprep.upto(m, f"r_{k}{hc}"))
                nc.scalar.activation(part["mid_" + k], dt if k == "d" else lg, ACT.Copy).then_inc(sprep.sem, 1)

            def take_BC(order, base, m, name, h):
                act.wait_ge(*((cur.sem, cur.upto(m - 1, "B")) if name == "B"
                              else (cur_C.sem, cur_C.upto(m - 1, "C"))))
                job_ready(order, base, name, h)
                nc.scalar.activation((Bst if name == "B" else Cst)[:, h * TH:(h + 1) * TH], job_ps[:, h, 0:TH],
                                     ACT.Copy).then_inc(job_read[h], 1)

            def keep_xn(n):
                act.wait_ge(vprep.sem, vprep.upto(n, "norm1"))
                nc.scalar.activation(xnz, xn, ACT.Copy).then_inc(z_in.sem, 1)

            def skip(n, c):
                act.wait_ge(cur.sem, cur.upto(n, "D"))
                act.wait_ge(gated.sem, gated.upto(n - 1, f"skip{c}"))
                act.wait_ge(vprep.sem, vprep.upto(n, f"silu{c}"))
                nc.scalar.activation(xsD[:, c, :], xs[:, c, :], ACT.Identity, scale=curD[:, c:c + 1]
                                     ).then_inc(skip_x.sem, 1)

            def take_z(order, base, c, h):
                job_ready(order, base, f"z{c}", h)
                nc.scalar.activation(thz[:, h, :], job_ps[:, h, 0:TH], ACT.Tanh, scale=0.5
                                     ).then_inc(z_tanh.sem, 1)

            def body(order, base, n):
                m = n + 1
                prep = "ms" in order
                for g in range(G):
                    decay_of(n, g)
                    if g == 0:
                        keep_xn(n)
                    if g < 3:
                        skip(n, g)
                    if g == 7:
                        skip(n, 3)
                    for c in range(KI):
                        for h in range(2):
                            if AT[f"z{c}"][h] + 1 == g:
                                take_z(order, base, c, h)
                    if not prep:
                        continue
                    if g == 3:
                        root(order, base, m)
                    for c in range(KI):
                        for h in range(2):
                            if AT[f"xi{c}"][h] + 1 == g:
                                take_xi(order, base, m, c, h)
                            if AT[f"dt{c}"][h] + 1 == g:
                                take_dt(order, base, m, c, h)
                    for h in range(2):
                        if AT["xp"][h] + 1 == g:
                            take_xp(order, base, h)
                        for name in "BC":
                            if AT[name][h] + 1 == g:
                                take_BC(order, base, m, name, h)
                    if g in TANH_AT:
                        tanh_conv(m, TANH_AT.index(g))
                    if g in SOFTPLUS_AT:
                        softplus(order, base, m, SOFTPLUS_AT.index(g))
                    for hc in range(2):
                        for i, k in enumerate("dx"):
                            if SPLIT_AT[hc][i] == g:
                                high(m, hc, k)
                            if SPLIT_AT[hc][2 + i] == g:
                                middle(m, hc, k)

            TANH_AT = [12, 17, 22, 26]
            SOFTPLUS_AT = [37, 52]
            SPLIT_AT = [(45, 47, 48, 49), (58, 60, 61, 62)]

            def prepare_first(base, m):
                o = PREP_PAIRS
                root(o, base, m)
                for c in range(KI):
                    for h in range(2):
                        take_xi(o, base, m, c, h)
                    tanh_conv(m, c)
                for h in range(2):
                    take_xp(o, base, h)
                for hc in range(2):
                    for c in (2 * hc, 2 * hc + 1):
                        for h in range(2):
                            take_dt(o, base, m, c, h)
                    softplus(o, base, m, hc)
                    if hc == 0:
                        for name in "BC":
                            for h in range(2):
                                take_BC(o, base, m, name, h)
                    for k in "dx":
                        high(m, hc, k)
                    for k in "dx":
                        middle(m, hc, k)

            def head(bk):
                for m in range(KD):
                    await_job(act, bk, ("pre1", m))
                    nc.scalar.activation(preh[:, m, :], abank(("pre1", m))[:, 0:SLOTS * LC], ACT.Silu
                                         ).then_inc(read_sem(("pre1", m)), 1)
                for m in range(KD):
                    await_job(act, bk, ("pre2", m))
                    nc.scalar.activation(hT[:, :, m, 0:LC],
                                         abank(("pre2", m))[:, 0:SLOTS * LC].rearrange("p (b t) -> p b t", b=SLOTS),
                                         ACT.Copy).then_inc(read_sem(("pre2", m)), 1)

            def finish(base, nl):
                pass

            def attend(bk):
                def from_bank(j, o, func, cols=512, **kw):
                    await_job(act, bk, j)
                    i = abank(j)[:, 0:cols]
                    if len(o.shape) == 3:
                        i = i.rearrange("p (a b) -> p a b", a=o.shape[1])
                    nc.scalar.activation(o, i, func, **kw).then_inc(read_sem(j), 1)

                def kp(k):
                    return slice(0, P if k == 0 else DC - P)

                act.wait_ge(block_scanned, bk + 1)
                for b in R4:
                    from_bank(("ms", b), rs[:, b, :], ACT.Ln, bias=EPS)
                for b in R4:
                    await_read(act, bk, ("ms", b))
                    nc.scalar.activation(rs[:, b, :], rs[:, b, :], ACT.Exp, scale=-0.5).then_inc(asc.sem, 1)
                from_bank(("cvar",), crs, ACT.Ln, cols=SLOTS * LC, bias=EPS)
                for b in R4:
                    from_bank(("var", b), rs[:, b, :], ACT.Ln, bias=EPS)
                await_read(act, bk, ("cvar",))
                nc.scalar.activation(crs, crs, ACT.Exp, scale=-0.5).then_inc(asc.sem, 1)
                for b in R4:
                    await_read(act, bk, ("var", b))
                    nc.scalar.activation(rs[:, b, :], rs[:, b, :], ACT.Exp, scale=-0.5).then_inc(asc.sem, 1)
                act.wait_ge(av.sem, av.upto(bk, "cn1"))
                for copy in range(2):
                    for k in range(KD):
                        nc.scalar.activation(cn2[kp(k), k, :, copy * LC:(copy + 1) * LC],
                                             cc[kp(k), k, :].rearrange("p (b t) -> p b t", b=SLOTS),
                                             ACT.Identity, bias=ln2_b[kp(k), k:k + 1]).then_inc(asc.sem, 1)
                for b in R4:
                    for k in range(KD):
                        act.wait_ge(av.sem, av.upto(bk, f"xn{b}{k}"))
                        nc.scalar.activation(xna[:, b, k, :], xna[:, b, k, :], ACT.Identity,
                                             bias=ln1_b[:, k:k + 1]).then_inc(asc.sem, 1)
                for m in range(KD):
                    from_bank(("k", m), kT[:, m, :], ACT.Copy, cols=SLOTS * LC)
                for b in R4:
                    for m in range(KD):
                        from_bank(("q", b, m), q[:, b, m, :], ACT.Copy, scale=HD ** -0.5)

                def turned(i):
                    b, m = units[i]
                    for r in range(4):
                        if i:
                            await_job(act, bk, ("pv", *units[i - 1]))
                        from_bank(("turn", b, m, r), pT[:, r, :], ACT.Copy)
                    from_bank(("pv", b, m), oT[:, b, m, :], ACT.Copy)

                for i, (b, m) in enumerate(units):
                    for r in range(4):
                        await_read(act, bk, ("score", b, m, r))
                        nc.scalar.activation(prob[:, m, r, :], prob[:, m, r, :], ACT.Exp).then_inc(asc.sem, 1)
                    if i:
                        turned(i - 1)
                turned(len(units) - 1)
                for b in R4:
                    from_bank(("var3", b), rs[:, b, :], ACT.Ln, bias=EPS)
                for b in R4:
                    await_read(act, bk, ("var3", b))
                    nc.scalar.activation(rs[:, b, :], rs[:, b, :], ACT.Exp, scale=-0.5).then_inc(asc.sem, 1)
                for b in R4:
                    for k in range(KD):
                        act.wait_ge(av.sem, av.upto(bk, f"yn{b}{k}"))
                        nc.scalar.activation(xna[:, b, k, :], xna[:, b, k, :], ACT.Identity,
                                             bias=ln3_b[:, k:k + 1]).then_inc(asc.sem, 1)
                for b in R4:
                    if b > 1:
                        await_job(act, bk, ("down", b - 2, 3))
                    for f in range(8):
                        from_bank(("up", b, f), hid[:, b % 2, f, :], ACT.Gelu, bias=b1_v[:, f:f + 1])

            act.wait_ge(cst_loaded, 64)
            nc.scalar.activation(negA[:, :, :], negA[:, :, :], ACT.Exp).then_inc(cst_exp, 1)
            act.wait_ge(cst_ready, 1)
            walk(act, prepare_first, body, finish, attend, head)

        @block.vector
        def _(dve):
            def job_ready(order, base, name, h):
                dve.wait_ge(job_done, pair_index(order, base, name) * 2 + (h + 1))

            def layer(n):
                return nc.s_assert_within((n >> 2) & 3, 0, L - 1, skip_runtime_bounds_check_because=IN_RANGE)

            def slot(n):
                return nc.s_assert_within(n & 3, 0, SLOTS - 1, skip_runtime_bounds_check_because=IN_RANGE)

            def h_of(n, k=None, t=slice(0, T)):
                v = hT[:, bass.ds(slot(n), 1), :, t] if k is None else hT[:, bass.ds(slot(n), 1), k, t]
                return v.rearrange("p a k t -> p (a k) t") if k is None else v.rearrange("p a t -> p (a t)")

            def make_input(n, g):
                if g == 0:
                    dve.wait_ge(cur.sem, cur.upto(n, "B"))
                dve.wait_ge(summed.sem, summed.before(n, g // QUAD - 1))
                dve.wait_ge(dtx_rep.sem, dtx_rep.before(n, g + 1))
                nc.vector.tensor_tensor(ring[:, g % PRING, :].rearrange("p (h t) -> p h t", h=2),
                                        dtx_ps[:, :, 0:TH], Brep.rearrange("p (h t) -> p h t", h=2),
                                        ALU.mult).then_inc(inp.sem, 1)

            def scan(n, g):
                dve.wait_ge(inp.sem, inp.before(n, g + 1))
                dve.wait_ge(decay.sem, decay.before(n, g + 1))
                s = ring[:, g % PRING, :]
                nc.vector.tensor_tensor_scan(s, dA[:, g % RING, :], s, 0.0, ALU.mult, ALU.add
                                             ).then_inc(state.sem, 1)

            def next_B(order, base, n, m):
                dve.wait_ge(inp.sem, inp.before(m))
                k = pair_index(order, base, "B")
                for h in range(2):
                    dve.wait_ge(job_read[h], k + 2)
                nc.vector.tensor_copy(Brep, Bst).then_inc(cur.sem, 1)

            def next_A_D(m):
                dve.wait_ge(decay.sem, decay.before(m))
                lay = layer(m)
                nc.vector.tensor_scalar(curA[:, :], negA[:, bass.ds(lay, 1), :].rearrange("p a g -> p (a g)"),
                                        1.0, None, ALU.mult).then_inc(cur.sem, 1)
                dve.wait_ge(skip_x.sem, skip_x.before(m))
                nc.vector.tensor_scalar(curD[:, :], Dall[:, bass.ds(lay, 1), :].rearrange("p a g -> p (a g)"),
                                        0.5, None, ALU.mult).then_inc(cur.sem, 1)

            def squares(m):
                dve.wait_ge(vprep.sem, vprep.before(m))
                nc.vector.tensor_tensor(square_low, h_of(m), h_of(m), ALU.mult).then_inc(vprep.sem, 1)

            def norm(m):
                dve.wait_ge(early_ready, m + 1)
                dve.wait_ge(z_in.sem, z_in.before(m))
                dve.wait_ge(sprep.sem, sprep.upto(m, "rstd"))
                for k in range(KD):
                    nc.vector.scalar_tensor_tensor(xn[:, k, :], h_of(m, k), norm_w[:, k:k + 1], rstd,
                                                   ALU.mult, ALU.mult).then_inc(vprep.sem, 1)

            def tap(order, base, m, c, i):
                if i == 0:
                    k = pair_index(order, base, f"xi{c}")
                    for h in range(2):
                        dve.wait_ge(job_read[h], k + 2)
                else:
                    dve.wait_ge(vprep.sem, vprep.upto(m, f"tap{i - 1}_{c}"))
                nc.vector.scalar_tensor_tensor(acc[:, c % 2, :], xpad[:, c % 2, i:i + T], taps[:, c, i:i + 1],
                                               acc[:, c % 2, :], ALU.mult, ALU.add).then_inc(vprep.sem, 1)

            def silu(m, c):
                dve.wait_ge(skip_x.sem, skip_x.upto(m - 1, c))
                dve.wait_ge(sprep.sem, sprep.upto(m, f"tanh{c}"))
                nc.vector.scalar_tensor_tensor(xs[:, c, :], th[:, c % 2, :], 1.0, acc[:, c % 2, :],
                                               ALU.add, ALU.mult).then_inc(vprep.sem, 1)

            def low(m, hc):
                dve.wait_ge(sprep.sem, sprep.upto(m, f"exp{hc}"))
                nc.vector.tensor_scalar(square_low, u, 1.0, -1.0, ALU.add, ALU.add).then_inc(vprep.sem, 1)

            def rest(m, hc):
                dve.wait_ge(vprep.sem, vprep.upto(m, f"low{hc}"))
                dve.wait_ge(sprep.sem, sprep.upto(m, f"ln{hc}"))
                nc.vector.tensor_tensor(u, u, square_low, ALU.subtract).then_inc(vprep.sem, 1)

            def guard(m, hc):
                nc.vector.scalar_tensor_tensor(lg, square_low, 0.0, lg, ALU.is_gt, ALU.mult
                                               ).then_inc(vprep.sem, 1)

            def dtx(m, hc):
                dve.wait_ge(pprep.sem, pprep.upto(m, f"dt{hc}"))
                nc.vector.scalar_tensor_tensor(lg, xs[:, 2 * hc:2 * hc + 2, :], 0.5, dt, ALU.mult, ALU.mult
                                               ).then_inc(vprep.sem, 1)

            def gate_z(order, base, n, c, h):
                t = slice(h * TH, (h + 1) * TH)
                job_ready(order, base, f"z{c}", h)
                dve.wait_ge(z_tanh.sem, z_tanh.before(n, 2 * c + h + 1))
                nc.vector.scalar_tensor_tensor(yg[:, c, t], thz[:, h, :], 1.0, job_ps[:, h, 0:TH],
                                               ALU.add, ALU.mult).then_inc(job_read[h], 1)
                if c == KI - 1 and h == 1:
                    nc.vector.sem_inc(zw_free, 1)

            def output(order_z, n, c):
                dve.wait_ge(skip_x.sem, skip_x.upto(n, c))
                dve.wait_ge(gated.sem, gated.before(n, 2 * c))
                dve.wait_ge(summed.sem, summed.before(n, QUAD * (c + 1)))
                nc.vector.tensor_tensor(yt.rearrange("p (h t) -> p h t", h=2), y_ps[:, :, 0:TH],
                                        xsD[:, c, :].rearrange("p (h t) -> p h t", h=2), ALU.add
                                        ).then_inc(gated.sem, 1)
                dve.wait_ge(gated.sem, gated.upto(n, f"skip{c}"))
                for h in range(2):
                    dve.wait_ge(job_read[h], order_z)
                nc.vector.tensor_tensor(yg[:, c, :], yt, yg[:, c, :], ALU.mult).then_inc(gated.sem, 1)

            def residual(order, base, n, mm, h):
                t = slice(h * TH, (h + 1) * TH)
                job_ready(order, base, f"out{mm}", h)
                v = h_of(n, mm, t)
                nc.vector.scalar_tensor_tensor(v, job_ps[:, h, 0:TH], 0.5, v, ALU.mult, ALU.add
                                               ).then_inc(job_read[h], 1)
                if mm == 1 and h == 1:
                    nc.vector.sem_inc(ow_free, 1)

            TAP_AT = [(9, 10, 11, 13), (14, 15, 16, 18), (19, 20, 21, 23), (23, 24, 25, 27)]
            DT_AT = [(40, 41, 42, 46), (54, 55, 56, 59)]

            def body(order, base, n):
                m = n + 1
                prep = "ms" in order
                for g in range(G):
                    make_input(n, g)
                    if g:
                        scan(n, g - 1)
                    for c in range(KI):
                        for h in range(2):
                            if AT[f"z{c}"][h] + 2 == g:
                                gate_z(order, base, n, c, h)
                    if g in (22, 38, 54):
                        c = (g - 22) // 16
                        output(pair_index(order, base, f"z{c}") + 2, n, c)
                    if "out0" in order:
                        if g == 6:
                            output(base + (1 - Z3_BACK), n - 1, 3)
                        for mm in range(KD):
                            for h in range(2):
                                if AT[f"out{mm}"][h] + 2 == g:
                                    residual(order, base, n - 1, mm, h)
                    if not prep:
                        continue
                    if g == 0:
                        squares(m)
                    if g == 5:
                        norm(m)
                    for c in range(KI):
                        for i in range(3):
                            if TAP_AT[c][i] == g:
                                tap(order, base, m, c, i)
                        if TAP_AT[c][3] == g:
                            silu(m, c)
                    for hc in range(2):
                        for i, f in enumerate((low, rest, guard, dtx)):
                            if DT_AT[hc][i] == g:
                                f(m, hc)
                if prep:
                    next_B(order, base, n, m)
                scan(n, G - 1)
                if prep:
                    next_A_D(m)

            Z3_BACK = len(BODY_PAIRS) - BODY_PAIRS.index("z3") - 1

            def prepare_first(base, m):
                o = PREP_PAIRS
                squares(m)
                norm(m)
                for c in range(KI):
                    for i in range(3):
                        tap(o, base, m, c, i)
                    silu(m, c)
                for hc in range(2):
                    for f in (low, rest, guard, dtx):
                        f(m, hc)
                next_B(o, base, m - 1, m)
                next_A_D(m)

            def head(bk):
                dve.wait_ge(h_loaded, bk * 64 + 64)
                await_read(dve, bk, ("pre2", 0))
                await_read(dve, bk, ("pre2", 1))

            def finish(base, nl):
                output(base + (1 - Z3_BACK), nl, 3)
                for mm in range(KD):
                    for h in range(2):
                        residual(OUTS, base, nl, mm, h)
                for h in range(2):
                    dve.wait_ge(job_read[h], base + 3)
                nc.vector.sem_inc(block_scanned, 1)

            def attend(bk):
                X = [[hT[:, b, k, LC:T] for k in range(KD)] for b in R4]

                def kp(k):
                    return slice(0, P if k == 0 else DC - P)

                def done(name):
                    dve.wait_ge(av.sem, av.upto(bk, name))

                for b in R4:
                    v = hT[:, b, :, LC:T]
                    nc.vector.tensor_tensor(sq[:, b, :, :], v, v, ALU.mult).then_inc(av.sem, 1)
                done(f"sq{SLOTS - 1}")
                for b in R4:
                    dve.wait_ge(asc.sem, asc.upto(bk, f"rs{b}"))
                    for k in range(KD):
                        nc.vector.scalar_tensor_tensor(X[b][k], X[b][k], fin_w[:, k:k + 1], rs[:, b, :],
                                                       ALU.mult, ALU.mult).then_inc(av.sem, 1)
                dve.wait_ge(ctx_loaded, bk * 32 + 32)
                await_job(dve, bk, ("cmean",))
                for k in range(KD):
                    i = nc.vector.tensor_tensor(cc[kp(k), k, :], ctxs[kp(k), k, :],
                                                abank(("cmean",))[kp(k), 0:SLOTS * LC], ALU.subtract)
                    i.then_inc(av.sem if k == 0 else read_sem(("cmean",)), 1)
                done("ccen0")
                await_read(dve, bk, ("cmean",))
                for k in range(KD):
                    nc.vector.tensor_tensor(csq[kp(k), k, :], cc[kp(k), k, :], cc[kp(k), k, :], ALU.mult
                                            ).then_inc(av.sem, 1)

                def centre(job, b, first):
                    await_job(dve, bk, (job, b))
                    for k in range(KD):
                        i = nc.vector.tensor_tensor(xna[:, b, k, :], X[b][k], abank((job, b)), ALU.subtract)
                        i.then_inc(av.sem if k == 0 else read_sem((job, b)), 1)
                    done(f"{first}{b}")
                    await_read(dve, bk, (job, b))
                    nc.vector.tensor_tensor(sq[:, b, :, :], xna[:, b, :, :], xna[:, b, :, :], ALU.mult
                                            ).then_inc(av.sem, 1)

                def scaled(b, w, rname):
                    dve.wait_ge(asc.sem, asc.upto(bk, f"{rname}{b}"))
                    for k in range(KD):
                        nc.vector.scalar_tensor_tensor(xna[:, b, k, :], xna[:, b, k, :], w[:, k:k + 1],
                                                       rs[:, b, :], ALU.mult, ALU.mult).then_inc(av.sem, 1)

                done(f"fin{SLOTS - 1}{KD - 1}")
                for b in R4:
                    centre("mean", b, "cen")
                dve.wait_ge(asc.sem, asc.upto(bk, "crs"))
                for k in range(KD):
                    nc.vector.scalar_tensor_tensor(cc[kp(k), k, :], cc[kp(k), k, :], ln2_w[kp(k), k:k + 1],
                                                   crs[kp(k), :], ALU.mult, ALU.mult).then_inc(av.sem, 1)
                done(f"csq_{SLOTS - 1}")
                for b in R4:
                    scaled(b, ln1_w, "rv")
                for b in R4:
                    j = ("v", b)
                    await_job(dve, bk, j)
                    nc.vector.tensor_tensor(Vbd[:, b, :, :], abank(j)[:, 0:D].rearrange("p (a d) -> p a d", d=32),
                                            v_mask.unsqueeze(1).broadcast_to([P, 8, 32]), ALU.mult
                                            ).then_inc(read_sem(j), 1)
                for b, m in units:
                    await_read(dve, bk, ("k", m))
                    nc.vector.tensor_tensor(Kbd[:, KD * b + m, :, :],
                                            kT[:, m, b * LC:(b + 1) * LC].unsqueeze(1).broadcast_to([P, 8, LC]),
                                            head_mask.unsqueeze(2).broadcast_to([P, 8, LC]), ALU.mult
                                            ).then_inc(av.sem, 1)

                def normaliser(i):
                    b, m, r = tiles[i]
                    dve.wait_ge(asc.sem, asc.upto(bk, f"e{i}"))
                    if i > 1:
                        done(f"rec{i - 2}")
                        dve.wait_ge(apl.sem, apl.upto(bk, f"p{i - 2}"))
                    nc.vector.tensor_reduce(den[:, i % 2, :], prob[:, m, r, :].rearrange("p (a k) -> p a k", a=8),
                                            AX.X, ALU.add).then_inc(av.sem, 1)
                    done(f"sum{i}")
                    nc.vector.reciprocal(rden[:, i % 2, :], den[:, i % 2, :]).then_inc(av.sem, 1)

                for i, (b, m, r) in enumerate(tiles):
                    j = ("score", b, m, r)
                    s = abank(j).rearrange("p (a k) -> p a k", a=8)
                    await_job(dve, bk, j)
                    nc.vector.tensor_reduce(mx[:, i % 2, :], s, AX.X, ALU.max).then_inc(av.sem, 1)
                    if b:
                        await_job(dve, bk, ("turn", b - 1, m, 3))
                    done(f"max{i}")
                    nc.vector.tensor_tensor(prob[:, m, r, :].rearrange("p (a k) -> p a k", a=8), s,
                                            mx[:, i % 2, :].unsqueeze(2).broadcast_to([P, 8, LC]), ALU.subtract
                                            ).then_inc(read_sem(j), 1)
                    if i:
                        normaliser(i - 1)
                normaliser(len(tiles) - 1)
                for b in R4:
                    for m in range(KD):
                        j = ("proj", b, m)
                        await_job(dve, bk, j)
                        nc.vector.scalar_tensor_tensor(X[b][m], abank(j), bproj[:, m:m + 1], X[b][m],
                                                       ALU.add, ALU.add).then_inc(read_sem(j), 1)
                for b in R4:
                    centre("mean3", b, "den")
                done(f"dsq{SLOTS - 1}")
                for b in R4:
                    scaled(b, ln3_w, "r3")
                for b in R4:
                    for r in range(4):
                        j = ("down", b, r)
                        dve.wait_ge(stored[r % 2], bk * 128 + (b * 2 + r // 2) * 16 + 16)
                        await_job(dve, bk, j)
                        nc.vector.tensor_copy(otile[:, r % 2, :], abank(j)[:, 0:D]).then_inc(read_sem(j), 1)

            dve.wait_ge(cst_loaded, 64)
            nc.vector.tensor_copy(spread[:, :, :], csts[:, 0:512].rearrange("p (j m) -> p j m", j=QUAD))
            dve.wait_ge(cst_exp, 1)
            nc.vector.tensor_scalar(negA[:, :, :], negA[:, :, :], -1.0, None, ALU.mult).then_inc(cst_neg, 1)
            dve.wait_ge(cst_neg, 1)
            for s in steps + [av, asc, apl]:
                nc.vector.sem_inc(s.sem, s.credit)
            for s in job_read + aread + [zw_free, ow_free]:
                nc.vector.sem_inc(s, 1)
            for s in list(stacked.values()) + stored:
                nc.vector.sem_inc(s, 16)
            nc.vector.sem_inc(cst_ready, 1)

            def head_and_pad(bk):
                head(bk)
                nc.vector.memset(xpad[:, :, 0:TAPS - 1], 0.0).then_inc(pad_ready, 1)
                dve.wait_ge(pad_ready, bk + 1)

            walk(dve, prepare_first, body, finish, attend, head_and_pad)

        @block.gpsimd
        def _(pool):
            def product(n, k):
                if k == 0:
                    pool.wait_ge(cur_C.sem, cur_C.upto(n, "C"))
                pool.wait_ge(state.sem, state.before(n, 2 * k + 2))
                a = 2 * k % PRING
                nc.gpsimd.tensor_tensor(ring[:, a:a + 2, :], ring[:, a:a + 2, :],
                                        Crep.unsqueeze(1).broadcast_to([P, 2, T]), ALU.mult
                                        ).then_inc(prod.sem, 1)

            def next_C(order, base, m):
                pool.wait_ge(prod.sem, prod.before(m))
                k = pair_index(order, base, "C")
                for h in range(2):
                    pool.wait_ge(job_read[h], k + 2)
                nc.gpsimd.tensor_tensor(Crep, Cst, csts[:, 1320:1321].broadcast_to([P, T]), ALU.mult
                                        ).then_inc(cur_C.sem, 1)

            def log(m, hc):
                pool.wait_ge(vprep.sem, vprep.upto(m, f"guard{hc}"))
                nc.gpsimd.tensor_tensor(lg, lg, u, ALU.add).then_inc(pprep.sem, 1)

            def make_dt(m, hc):
                pool.wait_ge(pprep.sem, pprep.upto(m, f"log{hc}"))
                nc.gpsimd.tensor_tensor(dt, rl, lg, ALU.add).then_inc(pprep.sem, 1)

            def remainder(m, hc, k):
                pool.wait_ge(sprep.sem, sprep.upto(m, f"hi_{k}{hc}"))
                v = dt if k == "d" else lg
                if k == "d":
                    pool.wait_ge(vprep.sem, vprep.upto(m, f"dtx{hc}"))
                nc.gpsimd.tensor_tensor(v, v, part["hi_" + k], ALU.subtract).then_inc(pprep.sem, 1)

            def last_part(m, hc, k):
                pool.wait_ge(sprep.sem, sprep.upto(m, f"mid_{k}{hc}"))
                v = dt if k == "d" else lg
                nc.gpsimd.tensor_tensor(part["lo_" + k], v, part["mid_" + k], ALU.subtract
                                        ).then_inc(pprep.sem, 1)

            PREP_AT = {"log0": 21, "dt0": 22, "r_d0": 23, "r_x0": 24, "lo_d0": 25, "lo_x0": 25,
                       "log1": 28, "dt1": 28, "r_d1": 29, "r_x1": 30, "lo_d1": 31, "lo_x1": 31}

            def prep_step(m, name):
                hc = int(name[-1])
                if name[:3] == "log":
                    log(m, hc)
                elif name[:2] == "dt":
                    make_dt(m, hc)
                elif name[:2] == "r_":
                    remainder(m, hc, name[2])
                else:
                    last_part(m, hc, name[3])

            def body(order, base, n):
                prep = "ms" in order
                for k in range(G // 2):
                    product(n, k)
                    if prep:
                        for name in POOL_PREP:
                            if PREP_AT[name] == k:
                                prep_step(n + 1, name)
                if prep:
                    next_C(order, base, n + 1)

            def prepare_first(base, m):
                for name in POOL_PREP:
                    prep_step(m, name)
                next_C(PREP_PAIRS, base, m)

            def attend(bk):
                for i, (b, m, r) in enumerate(tiles):
                    pool.wait_ge(av.sem, av.upto(bk, f"rec{i}"))
                    v = prob[:, m, r, :].rearrange("p (a k) -> p a k", a=8)
                    nc.gpsimd.tensor_tensor(v, v, rden[:, i % 2, :].unsqueeze(2).broadcast_to([P, 8, LC]),
                                            ALU.mult).then_inc(apl.sem, 1)

            pool.wait_ge(cst_ready, 1)
            walk(pool, prepare_first, body, lambda base, nl: None, attend, lambda bk: None)

        @block.sync
        def _(sp):
            def split_rows(dst, src):
                yield dst[:, 0, :], src[0:P, :]
                yield dst[0:DC - P, 1, :], src[P:DC, :]

            for dst, src in ((csts[:, :], cst), (avecs[:, :], avec), (negA[:, :, :], a_log), (Dall[:, :, :], d_par)):
                sp.dma_start(dst, src).then_inc(cst_loaded, 16)
            sp.wait_ge(cst_ready, 1)

            def stack(m, hc):
                for k in "dx":
                    sp.wait_ge(pprep.sem, pprep.upto(m, f"lo_{k}{hc}"))
                    for i, name in enumerate(("hi_", "mid_", "lo_")):
                        for qq in range(QUAD):
                            sp.dma_start(st[k][32 * i:32 * i + 32, hc, qq:8:QUAD, :],
                                         part[name + k][32 * qq:32 * qq + 32, :, :]).then_inc(stacked[k, hc], 16)

            with sp.Fori(0, BLOCKS) as bk:
                for i in range(2):
                    sp.wait_ge(stored[i], bk * 128 + 16)
                for b in range(SLOTS):
                    sp.dma_start(hT[:, b, :, LC:T],
                                 xT[bass.ds(bk * SLOTS + b, 1), :, :].rearrange("a (k p) t -> p (a k) t", p=P)
                                 ).then_inc(h_loaded, 16)
                mine = ctxT[:, bass.ds(bk * (SLOTS * LC), SLOTS * LC)]
                for dst, src in [*split_rows(ctxs, mine), *split_rows(pw1, pre_w1)]:
                    sp.dma_start(dst, src).then_inc(head_loaded, 16)
                sp.dma_start(pw2, pre_w2.rearrange("(k p) m -> p k m", p=P)).then_inc(head_loaded, 16)
                with sp.Fori(0, L) as lay:
                    m0, done = bk * STEPS + lay * SLOTS, bk * L + lay
                    sp.wait_ge(pad_ready, bk + 1)
                    sp.wait_ge(pprep.sem, pprep.before(m0))
                    sp.dma_start(lv[:, 0:NP], w_early[bass.ds(lay, 1), :, :].rearrange("a p m -> p (a m)")
                                 ).then_inc(early_loaded, 16)
                    sp.dma_start(ipx, ip_x[bass.ds(lay, 1), :, :].rearrange("a (k p) m -> p (a k) m", p=P)
                                 ).then_inc(early_loaded, 16)
                    sp.dma_start(xpw, xp_w[bass.ds(lay, 1), :, :].rearrange("a (k p) m -> p (a k) m", p=P)
                                 ).then_inc(early_loaded, 16)
                    sp.dma_start(dtw[0:DR, :], dt_w[bass.ds(lay, 1), :, :].rearrange("a r m -> r (a m)")
                                 ).then_inc(early_loaded, 16)
                    sp.wait_ge(early_loaded, done * 64 + 64)
                    sp.sem_inc(early_ready, SLOTS)
                    for hc in range(2):
                        stack(m0, hc)
                    sp.wait_ge(zw_free, m0 + 1)
                    sp.dma_start(ipz, ip_z[bass.ds(lay, 1), :, :].rearrange("a (k p) m -> p (a k) m", p=P)
                                 ).then_inc(z_loaded, 16)
                    sp.wait_ge(z_loaded, done * 16 + 16)
                    sp.sem_inc(zw_ready, SLOTS)
                    sp.wait_ge(ow_free, m0 + 1)
                    sp.dma_start(opw, op_w[bass.ds(lay, 1), :, :].rearrange("a (k p) m -> p (a k) m", p=P)
                                 ).then_inc(o_loaded, 16)
                    sp.wait_ge(o_loaded, done * 16 + 16)
                    sp.sem_inc(ow_ready, SLOTS)
                    with sp.Fori(1, SLOTS) as b:
                        for hc in range(2):
                            stack(m0 + b, hc)
                sp.wait_ge(block_scanned, bk + 1)
                for dst, src in split_rows(ctxs, mine):
                    sp.dma_start(dst, src).then_inc(ctx_loaded, 16)
                for dst, src in [*split_rows(wk_s, wk), *split_rows(wv_s, wv)]:
                    sp.dma_start(dst, src).then_inc(aw_loaded, 16)
                for dst, src in ((wq_s, wq), (wp_s, wp), (w1_s, w1), (w2_s, w2)):
                    sp.dma_start(dst, src.rearrange("(k p) m -> p k m", p=P)).then_inc(aw_loaded, 16)
                sp.dma_start(b2_s[0:1, :], b2).then_inc(aw_loaded, 16)
                for b in range(SLOTS):
                    for r in range(4):
                        await_read(sp, bk, ("down", b, r))
                        sp.dma_start(out[bass.ds(bk * SLOTS + b, 1), r * P:(r + 1) * P, :]
                                     .rearrange("a t d -> t (a d)"), otile[:, r % 2, :]).then_inc(stored[r % 2], 16)
            for i in range(2):
                sp.wait_ge(stored[i], BLOCKS * 128 + 16)


def _inputs(x, ctx_768, **w):
    import numpy as np

    def a(name):
        return np.asarray(w[name])

    def f(v):
        return np.ascontiguousarray(v)

    def cols(v, n=P):
        return np.moveaxis(v.reshape(-1, n, *v.shape[1:]), 1, 0).reshape(n, -1)

    L0, L1 = "L0_xattn_", "L1_xattn_"
    early = [np.concatenate([cols(a(L0 + "norm_w")[i]), cols(a(L0 + "conv_w")[i]), cols(a(L0 + "conv_b")[i]),
                             cols(a(L0 + "dt_proj_b")[i])], 1) for i in range(L)]
    p = np.arange(P)
    cst = np.zeros((P, 1448), np.float32)
    for j in range(QUAD):
        cst[0:96, j * P:(j + 1) * P] = (p[:96, None] % 32) == CH * j + p[None, :] // DS
        cst[:, 512 + 32 * j:512 + 32 * (j + 1)] = p[:32][None, :] == CH * j + p[:, None] // DS
    cst[0:XP, 640:768] = p[:XP, None] == DR + p[None, :] % DS
    cst[0:XP, 768:896] = p[:XP, None] == DR + DS + p[None, :] % DS
    cst[:, 896:1024] = p[:, None] == p[None, :]
    cst[:, 1024:1032] = p[:8][None, :] == p[:, None] // HD
    cst[:, 1032:1064] = p[:32][None, :] // HD == p[:, None] // LC
    cst[:, 1064:1192] = 1.0 / D
    cst[:, 1192:1320] = 1.0 / DC
    cst[:, 1320:1448] = 1.0
    av = np.zeros((P, 32), np.float32)
    for i, name in enumerate(("ln1_w", "ln1_b", "ln3_w", "ln3_b", "bproj")):
        av[:, 2 * i:2 * i + 2] = cols(a(L1 + name))
    av[:, 10:12] = cols(a(L0 + "final_norm_w"))
    av[:, 12:20] = cols(a(L1 + "b1"))
    for i, name in ((20, "ln2_w"), (22, "ln2_b")):
        av[:, i] = a(L1 + name)[0:P]
        av[0:DC - P, i + 1] = a(L1 + name)[P:]
    ipT = a(L0 + "in_proj_w").transpose(0, 2, 1)
    return {
        "xT": f(np.asarray(x).transpose(0, 2, 1)),
        "ctxT": f(np.asarray(ctx_768).transpose(2, 0, 1).reshape(DC, B * LC)),
        "w_early": f(np.stack(early)),
        "ip_x": f(ipT[:, :, 0:DI]), "ip_z": f(ipT[:, :, DI:]),
        "xp_w": f(a(L0 + "x_proj_w").transpose(0, 2, 1)),
        "dt_w": f(a(L0 + "dt_proj_w").transpose(0, 2, 1)),
        "op_w": f(a(L0 + "out_proj_w").transpose(0, 2, 1)),
        "a_log": f(a(L0 + "A_log").reshape(L, G, P).transpose(2, 0, 1)),
        "d_par": f(a(L0 + "D_param").reshape(L, KI, P).transpose(2, 0, 1)),
        "pre_w1": f(a(L0 + "pre_w1")), "pre_w2": f(a(L0 + "pre_w2")),
        "cst": cst, "avec": av,
        "wq": f(a(L1 + "Wq")), "wk": f(a(L1 + "Wkv")[:, 0:D]), "wv": f(a(L1 + "Wkv")[:, D:]),
        "wp": f(a(L1 + "Wproj")), "w1": f(a(L1 + "W1")), "w2": f(a(L1 + "W2")),
        "b2": f(a(L1 + "b2").reshape(1, D)),
    }


def kernel(**inputs):
    import concourse.bacc as _bacc
    from concourse.bass_utils import run_bass_kernel_spmd as _run

    nc = _bacc.Bacc("TRN2", target_bir_lowering=False, num_devices=1)
    arrays = _inputs(**inputs)
    aps = {k: nc.dram_tensor(k, v.shape, F32, kind="ExternalInput").ap() for k, v in arrays.items()}
    aps["out"] = nc.dram_tensor("out", (B, S, D), F32, kind="ExternalOutput").ap()
    program(nc, **aps)
    r = _run(nc, [arrays], core_ids=[0])
    return r.results[0]["out"]
```

```python
import concourse.bass as bass
from concourse import mybir
from contextlib import ExitStack

F32 = mybir.dt.float32
BF16 = mybir.dt.bfloat16
ALU = mybir.AluOpType
ACT = mybir.ActivationFunctionType
AX = mybir.AxisListType

P = 128
B, S, D = 16, 512, 256
LC, DC = 64, 192
L, DI, DS, TAPS, DR = 4, 512, 16, 4, 16
T = LC + S
TH = T // 2
KD = D // P
KI = DI // P
SLOTS = 4
BLOCKS = B // SLOTS
STEPS = L * SLOTS
CH = P // DS
G = DI // CH
GC = G // KI
QUAD = 4
RING = 4
PRING = 16
XP = DR + 2 * DS
HEADS, HD = 16, 16
HID = 4 * D
EPS = 1e-5
NP = KD + KI * TAPS + KI + KI
IN_RANGE = "a loop's count masked to the range"

PREP_PAIRS = ["ms", "xi0", "xi1", "xi2", "xi3", "xp", "dt0", "dt1", "B", "C", "dt2", "dt3"]
AT = {"ms": (2, 3), "xi0": (10, 11), "xi1": (12, 13), "out0": (14, 16), "xi2": (18, 19), "xi3": (20, 21),
      "out1": (22, 24), "z0": (26, 27), "xp": (29, 31), "dt0": (33, 34), "dt1": (35, 36), "z1": (38, 39),
      "B": (42, 43), "C": (44, 45), "z2": (48, 49), "dt2": (51, 52), "dt3": (53, 54), "z3": (57, 58)}
BODY_PAIRS = list(AT)
VECTOR_DT = ["seen", "sum", "less", "dt", "dtx"]
SCALAR_DT = ["exp", "ln", "hi_d", "hi_x", "mid_d", "mid_x"]
POOL_DT = ["r_d", "r_x", "lo_d", "lo_x"]
VECTOR_PREP = (["norm0", "norm1"]
               + [f"{s}{c}" for c in range(KI) for s in ("tap0_", "tap1_", "tap2_", "silu")] + VECTOR_DT)
SCALAR_PREP = ["square", "rstd", "tanh0", "tanh1", "tanh2", "tanh3"] + SCALAR_DT
SUM_BEHIND = 13
LEAD = 2
LOG_AT = (38, 5)
SPREAD_DT = {g: [g + 1 + LEAD] for g in range(G)}
for _a in LOG_AT:
    for _i, _groups in enumerate(([], [], [4], [5, 6], [7, 8])):
        SPREAD_DT[_a + 1 + _i] = [_a + _g for _g in _groups]
GATED = [f"{s}{c}" for c in range(KI) for s in ("skip", "gate")]


class Steps:

    def __init__(self, sem, names, credit=None):
        self.sem, self.names, self.per = sem, names, len(names)
        self.credit = 2 * self.per if credit is None else credit

    def upto(self, n, name):
        return self.before(n, self.names.index(name) + 1)

    def before(self, n, k=0):
        return n * self.per + (self.credit + k)


def program(nc, xT, ctxT, w_early, ip_x, ip_z, xp_w, dt_w, op_w, a_log, d_par, pre_w1, pre_w2, cst, cst_spread,
            cst_attention, avec,
            wq, wk, wv, wp, w1, w2, b2, out):
    ctx = ExitStack()
    with ctx:
        def sb(name, shape, dt=F32):
            return ctx.enter_context(nc.sbuf_tensor(name, shape, dt))

        def pb(name, shape):
            return ctx.enter_context(nc.psum_tensor(name, shape, F32))

        def sem(name):
            return ctx.enter_context(nc.semaphore(name))

        hT = sb("hT", [P, SLOTS, KD, T])
        csts = sb("csts", [P, 512])
        spread = sb("spread", [P, QUAD, P], BF16)
        sum_states = csts[:, 0:128].rearrange("p (j m) -> p j m", j=QUAD)
        sel_B = csts[:, 128:256]
        sel_C = csts[:, 256:384]
        ones_x = csts[:, 384:512]
        avecs = sb("avecs", [P, 32])
        ln1_w, ln1_b, ln3_w, ln3_b, bproj, fin_w = (avecs[:, 2 * i:2 * i + 2] for i in range(6))
        b1_v, ln2_w, ln2_b = avecs[:, 12:20], avecs[:, 20:22], avecs[:, 22:24]
        negA = sb("negA", [P, L, G])
        Dall = sb("Dall", [P, L, KI])
        curA = sb("curA", [P, 2, G])
        curD = sb("curD", [P, 2, KI])
        ARENA = 47100
        arena = sb("arena", [P, ARENA])
        at = [0]

        def view(*shape, dt=F32):
            n = 1
            for s in shape:
                n *= s
            words = n if dt == F32 else n // 2
            assert at[0] + words <= ARENA, at[0] + words
            v = arena[:, at[0]:at[0] + words]
            at[0] += words
            if dt != F32:
                v = v.bitcast(dt)
            if len(shape) == 2:
                v = v.rearrange("p (a b) -> p a b", a=shape[0])
            if len(shape) == 3:
                v = v.rearrange("p (a b c) -> p a b c", a=shape[0], b=shape[1])
            return v

        dA = view(RING, T)
        ring = view(PRING, T)
        st = {"d": view(2, 8, T, dt=BF16), "x": view(2, 8, T, dt=BF16)}
        xn = view(2, KD, T)
        th = view(T)
        rstd = th
        xpad = view(2, T + TAPS - 1 + 1)
        xs = view(2 * KI, T).rearrange("p (s c) t -> p s c t", s=2)
        xdbl = view(T)
        Brep, Crep = view(2, T), view(2, T)
        rl, u, lg, dt = view(2, T), view(2, T), view(2, T), view(2, T)
        seen = dt
        part = {k: view(2, T, dt=BF16) for k in ("hi_d", "mid_d", "lo_d", "hi_x", "mid_x", "lo_x")}
        yt = view(T)
        yg = view(KI, T)
        ipx = view(KD, DI)
        ipz = view(KD, DI)
        xpw = view(KI, XP)
        dtw = view(DI)
        opw = view(KI, D)
        lv = view(NP + 2)
        norm_w = lv[:, 0:KD]
        taps = lv[:, KD:KD + KI * TAPS].rearrange("p (c k) -> p c k", c=KI)
        conv_b = lv[:, KD + KI * TAPS:KD + KI * TAPS + KI]
        dt_b = lv[:, KD + KI * TAPS + KI:NP]
        assert at[0] <= ARENA
        at[0] = 0
        sq = view(SLOTS, KD, S)
        xna = view(SLOTS, KD, S)
        q = view(SLOTS, KD, S)
        rs = view(SLOTS, S)
        oT = sq
        ctxs = view(KD, SLOTS * LC)
        cc = view(KD, SLOTS * LC)
        csq = view(KD, SLOTS * LC)
        crs = view(SLOTS * LC)
        cn2 = view(KD, SLOTS, 2 * LC)
        kT = view(KD, SLOTS * LC)
        Kbd = view(SLOTS * KD, 8, LC)
        Vbd = view(SLOTS, 8, 32)
        prob = view(2, 4, 8 * LC)
        mx = view(2, 8)
        den = view(2, 8)
        rden = view(2, 8)
        pT = view(4, S)
        hid = view(2, 8, S)
        otile = view(2, D)
        wq_s, wk_s, wv_s, wp_s = view(KD, D), view(KD, D), view(KD, D), view(KD, D)
        w1_s = view(KD, HID)
        w2_s = view(8, D)
        b2_s = view(D)
        preh = view(KD, SLOTS * LC)
        acst = view(424)
        ident, one_row = acst[:, 0:128], acst[0:1, 128:256]
        ones_c = acst[:, 256:384]
        head_mask, v_mask = acst[:, 384:392], acst[:, 392:424]
        spread_f32 = arena[:, 0:QUAD * P]
        pw1, pw2 = wq_s, wk_s

        bank = [pb(f"bank{i}", [P, 2, 512]) for i in range(4)]
        dt_ps, dtx_ps, y_ps, job_ps = bank

        cst_loaded, cst_ready = sem("cst_loaded"), sem("cst_ready")
        cst_exp, cst_neg, pad_ready = sem("cst_exp"), sem("cst_neg"), sem("pad_ready")
        h_loaded, ctx_loaded, aw_loaded = sem("h_loaded"), sem("ctx_loaded"), sem("aw_loaded")
        early_loaded, z_loaded, o_loaded = sem("early_loaded"), sem("z_loaded"), sem("o_loaded")
        late_loaded, late_ready = sem("late_loaded"), sem("late_ready")
        early_ready, zw_ready, ow_ready = sem("early_ready"), sem("zw_ready"), sem("ow_ready")
        zw_free, ow_free = sem("zw_free"), sem("ow_free")
        stacked = {(k, h): sem(f"stacked_{k}{h}") for k in "dx" for h in range(2)}
        job_done = sem("job_done")
        job_read = [sem("job_read0"), sem("job_read1")]
        dt_rep = Steps(sem("dt_spread"), range(G))
        dtx_rep = Steps(sem("dtx_spread"), range(G))
        decay = Steps(sem("decay_ready"), range(G))
        inp = Steps(sem("input_ready"), range(G))
        state = Steps(sem("state_ready"), range(G))
        prod = Steps(sem("product_ready"), range(G // 2))
        summed = Steps(sem("states_summed"), range(G // QUAD))
        gated = Steps(sem("gated"), GATED)
        cur = Steps(sem("cur_ready"), ["A", "D"])
        z_tanh = Steps(sem("z_tanh"), range(2 * KI))
        vprep = Steps(sem("vector_prep"), VECTOR_PREP)
        sprep = Steps(sem("scalar_prep"), SCALAR_PREP)
        vdt = [vprep, Steps(sem("vector_late"), VECTOR_DT)]
        sdt = [sprep, Steps(sem("scalar_late"), SCALAR_DT)]
        pdt = [Steps(sem("pool_early"), POOL_DT), Steps(sem("pool_late"), POOL_DT)]
        block_scanned = sem("block_scanned")
        steps = [dt_rep, dtx_rep, decay, inp, state, prod, summed, gated, cur, z_tanh,
                 *vdt, *sdt, *pdt]

        jobs = [("pre1", 0), ("pre1", 1), ("pre2", 0), ("pre2", 1)]
        jobs += [("ms", b) for b in range(SLOTS)] + [("cmean",)]
        jobs += [("mean", b) for b in range(SLOTS)] + [("cvar",)]
        jobs += [("var", b) for b in range(SLOTS)]
        jobs += [("k", m) for m in range(KD)] + [("v", b) for b in range(SLOTS)]
        jobs += [("q", b, m) for b in range(SLOTS) for m in range(KD)]
        units = [(b, m) for b in range(SLOTS) for m in range(KD)]
        for i, (b, m) in enumerate(units):
            jobs += [("score", b, m, r) for r in range(4)]
            if i:
                pbm = units[i - 1]
                jobs += [("turn", *pbm, r) for r in range(4)] + [("pv", *pbm)]
        jobs += [("turn", *units[-1], r) for r in range(4)] + [("pv", *units[-1])]
        jobs += [("proj", b, m) for b in range(SLOTS) for m in range(KD)]
        jobs += [("mean3", b) for b in range(SLOTS)] + [("var3", b) for b in range(SLOTS)]
        for b in range(SLOTS):
            jobs += [("up", b, f) for f in range(8)]
            if b:
                jobs += [("down", b - 1, r) for r in range(4)]
        jobs += [("down", SLOTS - 1, r) for r in range(4)]
        number = {j: i for i, j in enumerate(jobs)}
        on_bank = [len(range(k, len(jobs), 8)) for k in range(8)]
        adone = sem("attention_job_done")
        aread = [sem(f"attention_job_read{i}") for i in range(8)]

        def abank(j):
            i = number[j] % 8
            return bank[i // 2][:, i % 2, :]

        def await_job(eng, bk, j):
            eng.wait_ge(adone, bk * len(jobs) + (number[j] + 1))

        def read_sem(j):
            return aread[number[j] % 8]

        def await_read(eng, bk, j):
            eng.wait_ge(read_sem(j), bk * on_bank[number[j] % 8] + (number[j] // 8 + 2))

        def await_bank(eng, bk, j):
            eng.wait_ge(read_sem(j), bk * on_bank[number[j] % 8] + (number[j] // 8 + 1))

        def await_reads(eng, bk, j, read):
            count = {number[j] % 8: number[j] // 8}
            for i in (number[x] for x in read):
                count[i % 8] = max(count.get(i % 8, 0), i // 8 + 1)
            for k, c in count.items():
                eng.wait_ge(aread[k], bk * on_bank[k] + (c + 1))

        R4 = range(SLOTS)
        tiles = [(b, m, r) for b, m in units for r in range(4)]
        av = Steps(sem("attention_vector"),
                   [f"sq{b}" for b in R4] + [f"fin{b}{k}" for b in R4 for k in range(KD)]
                   + ["ccen0", "csq0", "csq1"] + [f"{s}{b}" for b in R4 for s in ("cen", "csq_")]
                   + ["cn0", "cn1"] + [f"xn{b}{k}" for b in R4 for k in range(KD)]
                   + [f"kbd{b}{m}" for b, m in units]
                   + [f"{s}{i - (s != 'max')}" for i in range(33) for s in ("max", "sum", "rec")
                      if (i < 32 if s == "max" else i > 0)]
                   + [f"{s}{b}" for b in R4 for s in ("den", "dsq")]
                   + [f"yn{b}{k}" for b in R4 for k in range(KD)], 1)
        asc = Steps(sem("attention_scalar"),
                    [f"rs{b}" for b in R4] + ["crs"] + [f"rv{b}" for b in R4] + ["cb0", "cb1", "cb0d", "cb1d"]
                    + [f"xb{b}{k}" for b in R4 for k in range(KD)] + [f"e{i}" for i in range(32)]
                    + [f"r3{b}" for b in R4] + [f"yb{b}{k}" for b in R4 for k in range(KD)], 1)
        apl = Steps(sem("attention_pool"), [f"p{i}" for i in range(32)], 1)
        stored = [sem("stored0"), sem("stored1")]
        head_loaded = sem("head_loaded")

        def pair_index(order, base, name):
            return base + order.index(name)

        FIRST = [p for p in BODY_PAIRS if p[:3] != "out"]
        LAST = [p for p in BODY_PAIRS if p not in PREP_PAIRS]
        B_BACK = len(BODY_PAIRS) - BODY_PAIRS.index("B") - 1
        B_BACK_FIRST = len(PREP_PAIRS) - PREP_PAIRS.index("B") - 1

        OUTS = ["out0", "out1"]

        def walk(eng, prepare_first, body, finish, attend, head):
            with eng.Fori(0, BLOCKS) as bk:
                head(bk)
                n0, b0 = bk * STEPS, bk * (18 * STEPS)
                prepare_first(b0, n0)
                body(FIRST, b0 + 12, n0, 0)
                with eng.Fori(0, STEPS // 2 - 1) as it:
                    for odd in (1, 0):
                        done = it * 2 + (1 if odd else 2)
                        body(BODY_PAIRS, b0 + it * 36 + (28 if odd else 46), n0 + done, odd)
                body(LAST, b0 + (18 * STEPS - 8), n0 + (STEPS - 1), 1)
                finish(b0 + (18 * STEPS - 2), n0 + (STEPS - 1))
                attend(bk)

        block = ctx.enter_context(nc.Block())

        @block.tensor
        def _(pe):
            def spread_dt(n, g):
                c, j, qq = g // GC, (g % GC) // QUAD, g % QUAD
                if g % (G // 2) == 0:
                    pe.wait_ge(stacked["d", g // (G // 2)], (n + 1) * 192 + 16)
                pe.wait_ge(decay.sem, decay.before(n, g))
                for h in range(2):
                    i = nc.tensor.matmul(dt_ps[:, h, 0:TH], spread[0:96, j, :],
                                         st["d"][0:96, c // 2, (c % 2) * 4 + qq, h * TH:(h + 1) * TH],
                                         start=True, stop=True)
                i.then_inc(dt_rep.sem, 1)

            def spread_dtx(n, g):
                c, j, qq = g // GC, (g % GC) // QUAD, g % QUAD
                if g % (G // 2) == 0:
                    pe.wait_ge(stacked["x", g // (G // 2)], (n + 1) * 192 + 16)
                pe.wait_ge(inp.sem, inp.before(n, g))
                for h in range(2):
                    i = nc.tensor.matmul(dtx_ps[:, h, 0:TH], spread[0:96, j, :],
                                         st["x"][0:96, c // 2, (c % 2) * 4 + qq, h * TH:(h + 1) * TH],
                                         start=True, stop=True)
                i.then_inc(dtx_rep.sem, 1)

            def sum_quad(n, k, h):
                j = k % QUAD
                if h == 0:
                    pe.wait_ge(prod.sem, prod.before(n, 2 * k + 2))
                    if j == 0:
                        pe.wait_ge(gated.sem, gated.before(n, 2 * (k // QUAD) - 1))
                for qq in range(QUAD):
                    slot = (QUAD * k + qq) % PRING
                    i = nc.tensor.matmul(y_ps[32 * qq:32 * qq + 32, h, 0:TH], sum_states[:, j, :],
                                         ring[:, slot, h * TH:(h + 1) * TH],
                                         start=(j == 0), stop=(j == QUAD - 1))
                if h == 1:
                    i.then_inc(summed.sem, 1)

            def job(order, base, n, m, name, h, odd, piece=None):
                k = pair_index(order, base, name)
                t = slice(h * TH, (h + 1) * TH)
                o = job_ps[:, h, 0:TH]
                if piece != 1:
                    pe.wait_ge(job_read[h], k + 1)
                if name == "ms":
                    pe.wait_ge(sprep.sem, sprep.upto(m, "square"))
                    parts = [(ones_x, xn[:, 1 - odd, kk, t]) for kk in range(KD)]
                elif name[:2] == "xi":
                    c = int(name[2])
                    pe.wait_ge(early_ready, m + 1)
                    pe.wait_ge(vprep.sem, vprep.upto(m, "norm1"))
                    parts = [(ipx[:, kk, c * P:(c + 1) * P], xn[:, 1 - odd, kk, t]) for kk in range(KD)]
                elif name == "xp":
                    pe.wait_ge(late_ready, m + 1)
                    pe.wait_ge(vprep.sem, vprep.upto(m, "silu3"))
                    o = job_ps[0:XP, h, 0:TH]
                    parts = [(xpw[:, c, :], xs[:, 1 - odd, c, t]) for c in range(KI)]
                elif name[:2] == "dt":
                    c = int(name[2])
                    if c < 2:
                        pe.wait_ge(job_read[h], pair_index(order, base, "xp") + 2)
                    parts = [(dtw[0:DR, c * P:(c + 1) * P], xdbl[0:DR, t])]
                elif name in "BC":
                    parts = [((sel_B if name == "B" else sel_C)[0:XP, :], xdbl[0:XP, t])]
                elif name[0] == "z":
                    c = int(name[1])
                    pe.wait_ge(zw_ready, n + 1)
                    parts = [(ipz[:, kk, c * P:(c + 1) * P], xn[:, odd, kk, t]) for kk in range(KD)]
                else:
                    mm = int(name[3])
                    pe.wait_ge(ow_ready, n)
                    pe.wait_ge(gated.sem, gated.upto(n - 1, "gate3"))
                    parts = [(opw[:, c, mm * P:(mm + 1) * P], yg[:, c, t]) for c in range(KI)]
                for j, (lhs, rhs) in enumerate(parts):
                    if piece in (None, j // 2):
                        i = nc.tensor.matmul(o, lhs, rhs, start=j == 0, stop=j == len(parts) - 1)
                if piece != 0:
                    i.then_inc(job_done, 1)

            def body(order, base, n, odd):
                last, first = "ms" not in order, "out0" not in order
                for g in range(G):
                    for spread_to, groups in ((spread_dtx, [g + 1]), (spread_dt, SPREAD_DT[g])):
                        for to in groups:
                            if to < G:
                                spread_to(n, to)
                            elif not last:
                                spread_to(n + 1, to - G)
                    h = (g - SUM_BEHIND) % QUAD
                    if h < 2:
                        k = (g - SUM_BEHIND) // QUAD
                        if k >= 0:
                            sum_quad(n, k, h)
                        elif not first:
                            sum_quad(n - 1, G // QUAD + k, h)
                    for name in order:
                        for h in range(2):
                            if name == "xp" or name in OUTS:
                                if g - AT[name][h] in (0, 1):
                                    job(order, base, n, n + 1, name, h, odd, g - AT[name][h])
                            elif AT[name][h] == g:
                                job(order, base, n, n + 1, name, h, odd)

            def attention(bk):
                def product(j, parts, rows=slice(0, P), cols=512, read=()):
                    await_reads(pe, bk, j, read)
                    o = abank(j)[rows, 0:cols]
                    if len(parts[0][1].shape) == 3:
                        o = o.rearrange("p (a b) -> p a b", a=parts[0][1].shape[1])
                    for i, (lhs, rhs) in enumerate(parts):
                        last = nc.tensor.matmul(o, lhs, rhs, start=i == 0, stop=i == len(parts) - 1)
                    last.then_inc(adone, 1)

                def kp(k):
                    return slice(0, P if k == 0 else DC - P)

                X = [[hT[:, b, k, LC:T] for k in range(KD)] for b in R4]
                for b in R4:
                    pe.wait_ge(av.sem, av.upto(bk, f"sq{b}"))
                    product(("ms", b), [(ones_x, sq[:, b, k, :]) for k in range(KD)])
                pe.wait_ge(ctx_loaded, bk * 48 + 48)
                product(("cmean",), [(ones_c[kp(k), :], ctxs[kp(k), k, :]) for k in range(KD)], cols=SLOTS * LC)
                for b in R4:
                    pe.wait_ge(av.sem, av.upto(bk, f"fin{b}1"))
                    product(("mean", b), [(ones_x, X[b][k]) for k in range(KD)])
                pe.wait_ge(av.sem, av.upto(bk, "csq1"))
                product(("cvar",), [(ones_c[kp(k), :], csq[kp(k), k, :]) for k in range(KD)], cols=SLOTS * LC)
                for b in R4:
                    pe.wait_ge(av.sem, av.upto(bk, f"csq_{b}"))
                    product(("var", b), [(ones_x, sq[:, b, k, :]) for k in range(KD)])
                pe.wait_ge(aw_loaded, bk * 144 + 144)
                pe.wait_ge(asc.sem, asc.upto(bk, "cb1"))
                for m in range(KD):
                    product(("k", m), [(wk_s[kp(k), k, m * P:(m + 1) * P], cn2[kp(k), k, :, 0:LC])
                                       for k in range(KD)], cols=SLOTS * LC)
                pe.wait_ge(asc.sem, asc.upto(bk, "cb1d"))
                for b in R4:
                    product(("v", b), [(cn2[kp(k), k, b, :], wv_s[kp(k), k, :]) for k in range(KD)], cols=D)
                for b in R4:
                    pe.wait_ge(asc.sem, asc.upto(bk, f"xb{b}1"))
                    for m in range(KD):
                        product(("q", b, m), [(wq_s[:, k, m * P:(m + 1) * P], xna[:, b, k, :]) for k in range(KD)])

                def turn(b, m):
                    for r in range(4):
                        j = ("turn", b, m, r)
                        pe.wait_ge(apl.sem, apl.upto(bk, f"p{tiles.index((b, m, 3))}"))
                        await_bank(pe, bk, j)
                        for qb in range(4):
                            i = nc.tensor.matmul(abank(j)[:, qb * P:(qb + 1) * P],
                                                 prob[:, m, qb, r * P:(r + 1) * P], ident,
                                                 start=qb == 0, stop=qb == 3)
                        i.then_inc(adone, 1)
                    j = ("pv", b, m)
                    await_reads(pe, bk, j, [("v", b)] + [("turn", b, m, r) for r in range(4)])
                    for r in range(4):
                        i = nc.tensor.matmul(abank(j)[32 * r:32 * r + 32, :], Vbd[:, b, m * 4 + r, :],
                                             pT[:, r, :], start=True, stop=True)
                    i.then_inc(adone, 1)

                for i, (b, m) in enumerate(units):
                    for r in range(4):
                        pe.wait_ge(av.sem, av.upto(bk, f"kbd{b}{m}"))
                        product(("score", b, m, r),
                                [(q[:, b, m, r * P:(r + 1) * P], Kbd[:, KD * b + m, :, :])], read=[("q", b, m)])
                    if i:
                        turn(*units[i - 1])
                turn(*units[-1])
                for b in R4:
                    for m in range(KD):
                        product(("proj", b, m), [(wp_s[:, k, m * P:(m + 1) * P], oT[:, b, k, :]) for k in range(KD)],
                                read=[("pv", b, k) for k in range(KD)])
                for b in R4:
                    product(("mean3", b), [(ones_x, X[b][k]) for k in range(KD)],
                            read=[("proj", b, k) for k in range(KD)])
                for b in R4:
                    pe.wait_ge(av.sem, av.upto(bk, f"dsq{b}"))
                    product(("var3", b), [(ones_x, sq[:, b, k, :]) for k in range(KD)])

                def down(b):
                    for r in range(4):
                        j = ("down", b, r)
                        await_reads(pe, bk, j, [("up", b, f) for f in range(8)])
                        o, t = abank(j), slice(r * P, (r + 1) * P)
                        nc.tensor.matmul(o[:, 0:D], one_row, b2_s[0:1, :], start=True, stop=False)
                        for k in range(KD):
                            nc.tensor.matmul(o[:, k * P:(k + 1) * P], X[b][k][:, t], ident, start=False, stop=False)
                        for f in range(8):
                            i = nc.tensor.matmul(o[:, 0:D], hid[:, b % 2, f, t], w2_s[:, f, :],
                                                 start=False, stop=f == 7)
                        i.then_inc(adone, 1)

                for b in R4:
                    pe.wait_ge(asc.sem, asc.upto(bk, f"yb{b}1"))
                    for f in range(8):
                        product(("up", b, f), [(w1_s[:, k, f * P:(f + 1) * P], xna[:, b, k, :]) for k in range(KD)])
                    if b:
                        down(b - 1)
                down(SLOTS - 1)

            def head(bk):
                pe.wait_ge(head_loaded, bk * 80 + 80)
                for m in range(KD):
                    j = ("pre1", m)
                    await_bank(pe, bk, j)
                    for k, rows in ((0, P), (1, DC - P)):
                        i = nc.tensor.matmul(abank(j)[:, 0:SLOTS * LC], pw1[0:rows, k, m * P:(m + 1) * P],
                                             ctxs[0:rows, k, :], start=k == 0, stop=k == 1)
                    i.then_inc(adone, 1)
                for m in range(KD):
                    await_read(pe, bk, ("pre1", m))
                for m in range(KD):
                    j = ("pre2", m)
                    await_bank(pe, bk, j)
                    for k in range(KD):
                        i = nc.tensor.matmul(abank(j)[:, 0:SLOTS * LC], pw2[:, k, m * P:(m + 1) * P], preh[:, k, :],
                                             start=k == 0, stop=k == 1)
                    i.then_inc(adone, 1)

            def prepare_first(base, m):
                for name in PREP_PAIRS:
                    for h in range(2):
                        job(PREP_PAIRS, base, m, m, name, h, 1)
                spread_dtx(m, 0)
                for g in range(1 + LEAD):
                    spread_dt(m, g)

            def finish(base, nl):
                for k in range((G - SUM_BEHIND + QUAD - 1) // QUAD, G // QUAD):
                    for h in range(2):
                        sum_quad(nl, k, h)
                for name in OUTS:
                    for h in range(2):
                        job(OUTS, base, nl + 1, nl, name, h, 0)

            def attend(bk):
                pe.wait_ge(block_scanned, bk + 1)
                attention(bk)

            pe.wait_ge(cst_ready, 1)
            walk(pe, prepare_first, body, finish, attend, head)

        @block.scalar
        def _(act):
            def halves(v):
                return v.rearrange("p (h t) -> p h t", h=2)

            def job_ready(order, base, name, h):
                act.wait_ge(job_done, pair_index(order, base, name) * 2 + (h + 1))

            def decay_of(n, g, odd):
                if g == 0:
                    act.wait_ge(cur.sem, cur.upto(n, "A"))
                act.wait_ge(state.sem, state.before(n, g - RING + 1))
                act.wait_ge(dt_rep.sem, dt_rep.before(n, g + 1))
                nc.scalar.activation(halves(dA[:, g % RING, :]), dt_ps[:, :, 0:TH], ACT.Exp,
                                     scale=curA[:, odd, g:g + 1]).then_inc(decay.sem, 1)

            def squares(m, odd):
                slot = nc.s_assert_within(m & 3, 0, SLOTS - 1, skip_runtime_bounds_check_because=IN_RANGE)
                nc.scalar.activation(xn[:, odd, :, :],
                                     hT[:, bass.ds(slot, 1), :, :].rearrange("p a k t -> p (a k) t"), ACT.Square
                                     ).then_inc(sprep.sem, 1)

            def root_log(order, base, m):
                act.wait_ge(vprep.sem, vprep.before(m))
                for h in range(2):
                    job_ready(order, base, "ms", h)
                    nc.scalar.activation(rstd[:, h * TH:(h + 1) * TH], job_ps[:, h, 0:TH], ACT.Ln,
                                         bias=EPS).then_inc(job_read[h], 1)

            def root(order, base):
                k = pair_index(order, base, "ms")
                act.wait_ge(job_read[0], k + 2)
                act.wait_ge(job_read[1], k + 2)
                nc.scalar.activation(rstd, rstd, ACT.Exp, scale=-0.5).then_inc(sprep.sem, 1)

            def take_xi(order, base, m, c, h, odd):
                if h == 0:
                    act.wait_ge(vprep.sem, vprep.upto(m if c > 1 else m - 1, f"tap2_{(c + 2) % KI}"))
                    act.wait_ge(gated.sem, gated.upto(m - 2, f"skip{c}"))
                job_ready(order, base, f"xi{c}", h)
                nc.scalar.activation(xpad[:, c % 2, TAPS - 1 + h * TH:TAPS - 1 + (h + 1) * TH],
                                     job_ps[:, h, 0:TH], ACT.Copy)
                nc.scalar.activation(xs[:, odd, c, h * TH:(h + 1) * TH], job_ps[:, h, 0:TH], ACT.Identity,
                                     bias=conv_b[:, c:c + 1], scale=taps[:, c, TAPS - 1:TAPS]
                                     ).then_inc(job_read[h], 1)

            def tanh_conv(m, c, odd):
                act.wait_ge(vprep.sem, vprep.upto(m, f"tap2_{c}"))
                nc.scalar.activation(th, xs[:, odd, c, :], ACT.Tanh, scale=0.5).then_inc(sprep.sem, 1)

            def take_xp(order, base, h):
                job_ready(order, base, "xp", h)
                nc.scalar.activation(xdbl[0:XP, h * TH:(h + 1) * TH], job_ps[0:XP, h, 0:TH], ACT.Copy,
                                     scale=0.5).then_inc(job_read[h], 1)

            def take_dt(order, base, m, c, h):
                if h == 0 and c % 2 == 0:
                    v = vdt[1 - c // 2]
                    act.wait_ge(v.sem, v.upto(m if c else m - 1, "dt"))
                job_ready(order, base, f"dt{c}", h)
                t = slice(h * TH, (h + 1) * TH)
                nc.scalar.activation(u[:, c % 2, t], job_ps[:, h, 0:TH], ACT.Abs, bias=dt_b[:, c:c + 1])
                nc.scalar.activation(rl[:, c % 2, t], job_ps[:, h, 0:TH], ACT.Relu, bias=dt_b[:, c:c + 1]
                                     ).then_inc(job_read[h], 1)

            def exponential(read, hc):
                for h in range(2):
                    act.wait_ge(job_read[h], read)
                nc.scalar.activation(u, u, ACT.Exp, scale=-1.0).then_inc(sdt[hc].sem, 1)

            def logarithm(m, hc):
                s, p = sdt[hc], pdt[1 - hc]
                act.wait_ge(s.sem, s.upto(m, "exp"))
                act.wait_ge(p.sem, p.upto(m if hc else m - 1, "lo_x"))
                nc.scalar.activation(lg, u, ACT.Ln, bias=1.0).then_inc(s.sem, 1)

            def high(m, hc, k):
                if k == "d":
                    act.wait_ge(vdt[hc].sem, vdt[hc].upto(m, "dt"))
                else:
                    act.wait_ge(vdt[hc].sem, vdt[hc].upto(m, "dtx"))
                act.wait_ge(stacked[k, 1 - hc], (m + hc) * 192 + 16)
                nc.scalar.activation(part["hi_" + k], dt if k == "d" else lg, ACT.Copy).then_inc(sdt[hc].sem, 1)

            def middle(m, hc, k):
                act.wait_ge(pdt[hc].sem, pdt[hc].upto(m, f"r_{k}"))
                nc.scalar.activation(part["mid_" + k], dt if k == "d" else lg, ACT.Copy).then_inc(sdt[hc].sem, 1)

            def take_BC(order, base, m, name, h, odd):
                act.wait_ge(*((inp.sem, inp.before(m - 1)) if name == "B" else (prod.sem, prod.before(m - 1))))
                job_ready(order, base, name, h)
                nc.scalar.activation((Brep if name == "B" else Crep)[:, odd, h * TH:(h + 1) * TH],
                                     job_ps[:, h, 0:TH], ACT.Copy).then_inc(job_read[h], 1)

            def take_z(order, base, c, h):
                job_ready(order, base, f"z{c}", h)
                nc.scalar.activation(yg[:, c, h * TH:(h + 1) * TH], job_ps[:, h, 0:TH], ACT.Tanh, scale=0.5
                                     ).then_inc(z_tanh.sem, 1)

            TANH_AT = [16, 20, 24, 28]
            SPLIT_AT = [(44, 45, 48, 50), (12, 13, 16, 18)]

            def split(m, hc, i):
                (high, middle)[i // 2](m, hc, "dx"[i % 2])

            def body(order, base, n, odd):
                m = n + 1
                prep = "ms" in order
                for g in range(-LEAD, G):
                    if g + LEAD < G:
                        decay_of(n, g + LEAD, odd)
                    for c in range(KI):
                        for h in range(2):
                            if AT[f"z{c}"][h] + 1 == g:
                                take_z(order, base, c, h)
                    if g == 0 and prep:
                        squares(m, 1 - odd)
                    if g == 1:
                        exponential(base + (1 if "out0" not in order else 0), 1)
                    if g == LOG_AT[1]:
                        if prep:
                            root_log(order, base, m)
                        logarithm(n, 1)
                    if g == LOG_AT[1] + 1 and prep:
                        root(order, base)
                    for i in range(4):
                        if SPLIT_AT[1][i] == g:
                            split(n, 1, i)
                    if not prep:
                        continue
                    for c in range(KI):
                        for h in range(2):
                            if AT[f"xi{c}"][h] + 1 == g:
                                take_xi(order, base, m, c, h, 1 - odd)
                            if AT[f"dt{c}"][h] + 1 == g:
                                take_dt(order, base, m, c, h)
                    for h in range(2):
                        if AT["xp"][h] + 2 == g:
                            take_xp(order, base, h)
                        for name in "BC":
                            if AT[name][h] + 1 == g:
                                take_BC(order, base, m, name, h, 1 - odd)
                    if g in TANH_AT:
                        tanh_conv(m, TANH_AT.index(g), 1 - odd)
                    if g == AT["dt1"][1] + 1:
                        exponential(pair_index(order, base, "dt1") + 2, 0)
                    if g == LOG_AT[0]:
                        logarithm(m, 0)
                    for i in range(4):
                        if SPLIT_AT[0][i] == g:
                            split(m, 0, i)

            def prepare_first(base, m):
                o = PREP_PAIRS
                squares(m, 0)
                root_log(o, base, m)
                root(o, base)
                for c in range(KI):
                    for h in range(2):
                        take_xi(o, base, m, c, h, 0)
                    tanh_conv(m, c, 0)
                for h in range(2):
                    take_xp(o, base, h)
                for c in range(2):
                    for h in range(2):
                        take_dt(o, base, m, c, h)
                exponential(pair_index(o, base, "dt1") + 2, 0)
                logarithm(m, 0)
                for name in "BC":
                    for h in range(2):
                        take_BC(o, base, m, name, h, 0)
                for i in range(4):
                    split(m, 0, i)
                for c in (2, 3):
                    for h in range(2):
                        take_dt(o, base, m, c, h)

            def head(bk):
                for m in range(KD):
                    await_job(act, bk, ("pre1", m))
                    nc.scalar.activation(preh[:, m, :], abank(("pre1", m))[:, 0:SLOTS * LC], ACT.Silu
                                         ).then_inc(read_sem(("pre1", m)), 1)
                for m in range(KD):
                    await_job(act, bk, ("pre2", m))
                    nc.scalar.activation(hT[:, :, m, 0:LC],
                                         abank(("pre2", m))[:, 0:SLOTS * LC].rearrange("p (b t) -> p b t", b=SLOTS),
                                         ACT.Copy).then_inc(read_sem(("pre2", m)), 1)
                act.wait_ge(h_loaded, bk * 64 + 64)
                await_read(act, bk, ("pre2", 0))
                await_read(act, bk, ("pre2", 1))

            def finish(base, nl):
                pass

            def attend(bk):
                def from_bank(j, o, func, cols=512, **kw):
                    await_job(act, bk, j)
                    i = abank(j)[:, 0:cols]
                    if len(o.shape) == 3:
                        i = i.rearrange("p (a b) -> p a b", a=o.shape[1])
                    nc.scalar.activation(o, i, func, **kw).then_inc(read_sem(j), 1)

                def kp(k):
                    return slice(0, P if k == 0 else DC - P)

                act.wait_ge(block_scanned, bk + 1)
                for b in R4:
                    from_bank(("ms", b), rs[:, b, :], ACT.Ln, bias=EPS)
                for b in R4:
                    await_read(act, bk, ("ms", b))
                    nc.scalar.activation(rs[:, b, :], rs[:, b, :], ACT.Exp, scale=-0.5).then_inc(asc.sem, 1)
                from_bank(("cvar",), crs, ACT.Ln, cols=SLOTS * LC, bias=EPS)
                for b in R4:
                    from_bank(("var", b), rs[:, b, :], ACT.Ln, bias=EPS)
                await_read(act, bk, ("cvar",))
                nc.scalar.activation(crs, crs, ACT.Exp, scale=-0.5).then_inc(asc.sem, 1)
                for b in R4:
                    await_read(act, bk, ("var", b))
                    nc.scalar.activation(rs[:, b, :], rs[:, b, :], ACT.Exp, scale=-0.5).then_inc(asc.sem, 1)
                act.wait_ge(av.sem, av.upto(bk, "cn1"))
                for copy in range(2):
                    for k in range(KD):
                        nc.scalar.activation(cn2[kp(k), k, :, copy * LC:(copy + 1) * LC],
                                             cc[kp(k), k, :].rearrange("p (b t) -> p b t", b=SLOTS),
                                             ACT.Identity, bias=ln2_b[kp(k), k:k + 1]).then_inc(asc.sem, 1)
                for b in R4:
                    for k in range(KD):
                        act.wait_ge(av.sem, av.upto(bk, f"xn{b}{k}"))
                        nc.scalar.activation(xna[:, b, k, :], xna[:, b, k, :], ACT.Identity,
                                             bias=ln1_b[:, k:k + 1]).then_inc(asc.sem, 1)
                for m in range(KD):
                    from_bank(("k", m), kT[:, m, :], ACT.Copy, cols=SLOTS * LC)
                for b in R4:
                    for m in range(KD):
                        from_bank(("q", b, m), q[:, b, m, :], ACT.Copy, scale=HD ** -0.5)

                def turned(i):
                    b, m = units[i]
                    for r in range(4):
                        if i:
                            await_job(act, bk, ("pv", *units[i - 1]))
                        from_bank(("turn", b, m, r), pT[:, r, :], ACT.Copy)
                    from_bank(("pv", b, m), oT[:, b, m, :], ACT.Copy)

                for i, (b, m) in enumerate(units):
                    for r in range(4):
                        await_read(act, bk, ("score", b, m, r))
                        nc.scalar.activation(prob[:, m, r, :], prob[:, m, r, :], ACT.Exp).then_inc(asc.sem, 1)
                    if i:
                        turned(i - 1)
                turned(len(units) - 1)
                for b in R4:
                    from_bank(("var3", b), rs[:, b, :], ACT.Ln, bias=EPS)
                for b in R4:
                    await_read(act, bk, ("var3", b))
                    nc.scalar.activation(rs[:, b, :], rs[:, b, :], ACT.Exp, scale=-0.5).then_inc(asc.sem, 1)
                for b in R4:
                    for k in range(KD):
                        act.wait_ge(av.sem, av.upto(bk, f"yn{b}{k}"))
                        nc.scalar.activation(xna[:, b, k, :], xna[:, b, k, :], ACT.Identity,
                                             bias=ln3_b[:, k:k + 1]).then_inc(asc.sem, 1)
                for b in R4:
                    if b > 1:
                        await_job(act, bk, ("down", b - 2, 3))
                    for f in range(8):
                        from_bank(("up", b, f), hid[:, b % 2, f, :], ACT.Gelu, bias=b1_v[:, f:f + 1])

            act.wait_ge(cst_loaded, 80)
            nc.scalar.activation(negA[:, :, :], negA[:, :, :], ACT.Exp).then_inc(cst_exp, 1)
            act.wait_ge(cst_ready, 1)
            walk(act, prepare_first, body, finish, attend, head)

        @block.vector
        def _(dve):
            def job_ready(order, base, name, h):
                dve.wait_ge(job_done, pair_index(order, base, name) * 2 + (h + 1))

            def layer(n):
                return nc.s_assert_within((n >> 2) & 3, 0, L - 1, skip_runtime_bounds_check_because=IN_RANGE)

            def slot(n):
                return nc.s_assert_within(n & 3, 0, SLOTS - 1, skip_runtime_bounds_check_because=IN_RANGE)

            def h_of(n, k=None, t=slice(0, T)):
                v = hT[:, bass.ds(slot(n), 1), :, t] if k is None else hT[:, bass.ds(slot(n), 1), k, t]
                return v.rearrange("p a k t -> p (a k) t") if k is None else v.rearrange("p a t -> p (a t)")

            def make_input(n, g, odd, base, b_back):
                if g == 0:
                    for h in range(2):
                        dve.wait_ge(job_read[h], base + (1 - b_back))
                dve.wait_ge(summed.sem, summed.before(n, (g - PRING) // QUAD + 1))
                dve.wait_ge(dtx_rep.sem, dtx_rep.before(n, g + 1))
                nc.vector.tensor_tensor(ring[:, g % PRING, :].rearrange("p (h t) -> p h t", h=2),
                                        dtx_ps[:, :, 0:TH], Brep[:, odd, :].rearrange("p (h t) -> p h t", h=2),
                                        ALU.mult).then_inc(inp.sem, 1)

            def scan(n, g):
                dve.wait_ge(inp.sem, inp.before(n, g + 1))
                dve.wait_ge(decay.sem, decay.before(n, g + 1))
                s = ring[:, g % PRING, :]
                nc.vector.tensor_tensor_scan(s, dA[:, g % RING, :], s, 0.0, ALU.mult, ALU.add
                                             ).then_inc(state.sem, 1)

            def next_A_D(m, odd):
                lay = layer(m)
                dve.wait_ge(decay.sem, decay.before(m - 1))
                nc.vector.tensor_scalar(curA[:, odd, :], negA[:, bass.ds(lay, 1), :].rearrange("p a g -> p (a g)"),
                                        1.0, None, ALU.mult).then_inc(cur.sem, 1)
                dve.wait_ge(gated.sem, gated.before(m - 1))
                nc.vector.tensor_scalar(curD[:, odd, :], Dall[:, bass.ds(lay, 1), :].rearrange("p a g -> p (a g)"),
                                        0.5, None, ALU.mult).then_inc(cur.sem, 1)

            def norm(m, k, odd):
                if k == 0:
                    dve.wait_ge(early_ready, m + 1)
                    dve.wait_ge(sprep.sem, sprep.upto(m, "rstd"))
                nc.vector.scalar_tensor_tensor(xn[:, odd, k, :], h_of(m, k), norm_w[:, k:k + 1], rstd,
                                               ALU.mult, ALU.mult).then_inc(vprep.sem, 1)

            def tap(order, base, m, c, i, odd):
                if i == 0:
                    k = pair_index(order, base, f"xi{c}")
                    for h in range(2):
                        dve.wait_ge(job_read[h], k + 2)
                else:
                    dve.wait_ge(vprep.sem, vprep.upto(m, f"tap{i - 1}_{c}"))
                nc.vector.scalar_tensor_tensor(xs[:, odd, c, :], xpad[:, c % 2, i:i + T], taps[:, c, i:i + 1],
                                               xs[:, odd, c, :], ALU.mult, ALU.add).then_inc(vprep.sem, 1)

            def silu(m, c, odd):
                dve.wait_ge(sprep.sem, sprep.upto(m, f"tanh{c}"))
                nc.vector.scalar_tensor_tensor(xs[:, odd, c, :], th, 1.0, xs[:, odd, c, :],
                                               ALU.add, ALU.mult).then_inc(vprep.sem, 1)

            def seen_of(m, hc, odd):
                p = pdt[1 - hc]
                dve.wait_ge(p.sem, p.upto(m if hc else m - 1, "lo_d"))
                dve.wait_ge(sdt[hc].sem, sdt[hc].upto(m, "exp"))
                nc.vector.tensor_scalar(seen, u, 1.0, -1.0, ALU.add, ALU.add).then_inc(vdt[hc].sem, 1)

            def sum_of(m, hc, odd):
                dve.wait_ge(sdt[hc].sem, sdt[hc].upto(m, "exp"))
                nc.vector.tensor_tensor(rl, rl, u, ALU.add).then_inc(vdt[hc].sem, 1)

            def less(m, hc, odd):
                dve.wait_ge(vdt[hc].sem, vdt[hc].upto(m, "seen"))
                dve.wait_ge(sdt[hc].sem, sdt[hc].upto(m, "ln"))
                nc.vector.scalar_tensor_tensor(lg, lg, 0.0, seen, ALU.max, ALU.subtract).then_inc(vdt[hc].sem, 1)

            def make_dt(m, hc, odd):
                dve.wait_ge(vdt[hc].sem, vdt[hc].upto(m, "less"))
                nc.vector.scalar_tensor_tensor(dt, lg, 0.0, rl, ALU.min, ALU.add).then_inc(vdt[hc].sem, 1)

            def dtx(m, hc, odd):
                dve.wait_ge(vdt[hc].sem, vdt[hc].upto(m, "dt"))
                nc.vector.scalar_tensor_tensor(lg, xs[:, odd, 2 * hc:2 * hc + 2, :], 0.5, dt, ALU.mult, ALU.mult
                                               ).then_inc(vdt[hc].sem, 1)

            def gate_z(order, base, n, c, h):
                t = slice(h * TH, (h + 1) * TH)
                job_ready(order, base, f"z{c}", h)
                dve.wait_ge(z_tanh.sem, z_tanh.before(n, 2 * c + h + 1))
                nc.vector.scalar_tensor_tensor(yg[:, c, t], yg[:, c, t], 1.0, job_ps[:, h, 0:TH],
                                               ALU.add, ALU.mult).then_inc(job_read[h], 1)
                if c == KI - 1 and h == 1:
                    nc.vector.sem_inc(zw_free, 1)

            def output(z_read, n, c, odd):
                dve.wait_ge(cur.sem, cur.upto(n, "D"))
                dve.wait_ge(gated.sem, gated.before(n, 2 * c))
                dve.wait_ge(summed.sem, summed.before(n, QUAD * (c + 1)))
                nc.vector.scalar_tensor_tensor(yt.rearrange("p (h t) -> p h t", h=2),
                                               xs[:, odd, c, :].rearrange("p (h t) -> p h t", h=2),
                                               curD[:, odd, c:c + 1], y_ps[:, :, 0:TH], ALU.mult, ALU.add
                                               ).then_inc(gated.sem, 1)
                dve.wait_ge(gated.sem, gated.upto(n, f"skip{c}"))
                for h in range(2):
                    dve.wait_ge(job_read[h], z_read)
                nc.vector.tensor_tensor(yg[:, c, :], yt, yg[:, c, :], ALU.mult).then_inc(gated.sem, 1)

            def residual(order, base, n, mm, h):
                t = slice(h * TH, (h + 1) * TH)
                job_ready(order, base, f"out{mm}", h)
                v = h_of(n, mm, t)
                nc.vector.scalar_tensor_tensor(v, job_ps[:, h, 0:TH], 0.5, v, ALU.mult, ALU.add
                                               ).then_inc(job_read[h], 1)
                if mm == 1 and h == 1:
                    nc.vector.sem_inc(ow_free, 1)

            OUTPUT_AT = [29, 43, 59, 75]
            TAP_AT = [(13, 14, 15, 17), (17, 18, 19, 21), (21, 22, 23, 25), (25, 26, 27, 29)]
            DT_AT = [(39, 40, 42, 43, 44), (4, 6, 10, 11, 12)]

            def body(order, base, n, odd):
                m = n + 1
                prep, first = "ms" in order, "out0" not in order
                for g in range(G):
                    make_input(n, g, odd, base, B_BACK_FIRST if first else B_BACK)
                    if g:
                        scan(n, g - 1)
                    for c in range(KI):
                        for h in range(2):
                            if AT[f"z{c}"][h] + 2 == g:
                                gate_z(order, base, n, c, h)
                    if g in OUTPUT_AT[0:3]:
                        c = OUTPUT_AT.index(g)
                        output(pair_index(order, base, f"z{c}") + 2, n, c, odd)
                    if not first:
                        if g == OUTPUT_AT[3] - G:
                            output(base + 1, n - 1, 3, 1 - odd)
                        for mm in range(KD):
                            for h in range(2):
                                if AT[f"out{mm}"][h] + 3 == g:
                                    residual(order, base, n - 1, mm, h)
                    for i, f in enumerate((seen_of, sum_of, less, make_dt, dtx)):
                        if DT_AT[1][i] == g:
                            f(n, 1, odd)
                    if not prep:
                        continue
                    if g in (8, 9):
                        norm(m, g - 8, 1 - odd)
                    if g == 40:
                        next_A_D(m, 1 - odd)
                    for c in range(KI):
                        for i in range(3):
                            if TAP_AT[c][i] == g:
                                tap(order, base, m, c, i, 1 - odd)
                        if TAP_AT[c][3] == g:
                            silu(m, c, 1 - odd)
                    for i, f in enumerate((seen_of, sum_of, less, make_dt, dtx)):
                        if DT_AT[0][i] == g:
                            f(m, 0, 1 - odd)
                scan(n, G - 1)

            def prepare_first(base, m):
                o = PREP_PAIRS
                for k in range(KD):
                    norm(m, k, 0)
                next_A_D(m, 0)
                for c in range(KI):
                    for i in range(3):
                        tap(o, base, m, c, i, 0)
                    silu(m, c, 0)
                for f in (seen_of, sum_of, less, make_dt, dtx):
                    f(m, 0, 0)

            def head(bk):
                dve.wait_ge(h_loaded, bk * 64 + 64)
                await_read(dve, bk, ("pre2", 0))
                await_read(dve, bk, ("pre2", 1))

            def finish(base, nl):
                output(base + 1, nl, 3, 1)
                for mm in range(KD):
                    for h in range(2):
                        residual(OUTS, base, nl, mm, h)
                for h in range(2):
                    dve.wait_ge(job_read[h], base + 3)
                nc.vector.sem_inc(block_scanned, 1)

            def attend(bk):
                X = [[hT[:, b, k, LC:T] for k in range(KD)] for b in R4]

                def kp(k):
                    return slice(0, P if k == 0 else DC - P)

                def done(name):
                    dve.wait_ge(av.sem, av.upto(bk, name))

                for b in R4:
                    v = hT[:, b, :, LC:T]
                    nc.vector.tensor_tensor(sq[:, b, :, :], v, v, ALU.mult).then_inc(av.sem, 1)
                done(f"sq{SLOTS - 1}")
                for b in R4:
                    dve.wait_ge(asc.sem, asc.upto(bk, f"rs{b}"))
                    for k in range(KD):
                        nc.vector.scalar_tensor_tensor(X[b][k], X[b][k], fin_w[:, k:k + 1], rs[:, b, :],
                                                       ALU.mult, ALU.mult).then_inc(av.sem, 1)
                dve.wait_ge(ctx_loaded, bk * 48 + 48)
                await_job(dve, bk, ("cmean",))
                for k in range(KD):
                    i = nc.vector.tensor_tensor(cc[kp(k), k, :], ctxs[kp(k), k, :],
                                                abank(("cmean",))[kp(k), 0:SLOTS * LC], ALU.subtract)
                    i.then_inc(av.sem if k == 0 else read_sem(("cmean",)), 1)
                done("ccen0")
                await_read(dve, bk, ("cmean",))
                for k in range(KD):
                    nc.vector.tensor_tensor(csq[kp(k), k, :], cc[kp(k), k, :], cc[kp(k), k, :], ALU.mult
                                            ).then_inc(av.sem, 1)

                def centre(job, b, first):
                    await_job(dve, bk, (job, b))
                    for k in range(KD):
                        i = nc.vector.tensor_tensor(xna[:, b, k, :], X[b][k], abank((job, b)), ALU.subtract)
                        i.then_inc(av.sem if k == 0 else read_sem((job, b)), 1)
                    done(f"{first}{b}")
                    await_read(dve, bk, (job, b))
                    nc.vector.tensor_tensor(sq[:, b, :, :], xna[:, b, :, :], xna[:, b, :, :], ALU.mult
                                            ).then_inc(av.sem, 1)

                def scaled(b, w, rname):
                    dve.wait_ge(asc.sem, asc.upto(bk, f"{rname}{b}"))
                    for k in range(KD):
                        nc.vector.scalar_tensor_tensor(xna[:, b, k, :], xna[:, b, k, :], w[:, k:k + 1],
                                                       rs[:, b, :], ALU.mult, ALU.mult).then_inc(av.sem, 1)

                done(f"fin{SLOTS - 1}{KD - 1}")
                for b in R4:
                    centre("mean", b, "cen")
                dve.wait_ge(asc.sem, asc.upto(bk, "crs"))
                for k in range(KD):
                    nc.vector.scalar_tensor_tensor(cc[kp(k), k, :], cc[kp(k), k, :], ln2_w[kp(k), k:k + 1],
                                                   crs[kp(k), :], ALU.mult, ALU.mult).then_inc(av.sem, 1)
                done(f"csq_{SLOTS - 1}")
                for b in R4:
                    scaled(b, ln1_w, "rv")
                for b in R4:
                    j = ("v", b)
                    await_job(dve, bk, j)
                    nc.vector.tensor_tensor(Vbd[:, b, :, :], abank(j)[:, 0:D].rearrange("p (a d) -> p a d", d=32),
                                            v_mask.unsqueeze(1).broadcast_to([P, 8, 32]), ALU.mult
                                            ).then_inc(read_sem(j), 1)
                for b, m in units:
                    await_read(dve, bk, ("k", m))
                    nc.vector.tensor_tensor(Kbd[:, KD * b + m, :, :],
                                            kT[:, m, b * LC:(b + 1) * LC].unsqueeze(1).broadcast_to([P, 8, LC]),
                                            head_mask.unsqueeze(2).broadcast_to([P, 8, LC]), ALU.mult
                                            ).then_inc(av.sem, 1)

                def normaliser(i):
                    b, m, r = tiles[i]
                    dve.wait_ge(asc.sem, asc.upto(bk, f"e{i}"))
                    if i > 1:
                        done(f"rec{i - 2}")
                        dve.wait_ge(apl.sem, apl.upto(bk, f"p{i - 2}"))
                    nc.vector.tensor_reduce(den[:, i % 2, :], prob[:, m, r, :].rearrange("p (a k) -> p a k", a=8),
                                            AX.X, ALU.add).then_inc(av.sem, 1)
                    done(f"sum{i}")
                    nc.vector.reciprocal(rden[:, i % 2, :], den[:, i % 2, :]).then_inc(av.sem, 1)

                for i, (b, m, r) in enumerate(tiles):
                    j = ("score", b, m, r)
                    s = abank(j).rearrange("p (a k) -> p a k", a=8)
                    await_job(dve, bk, j)
                    nc.vector.tensor_reduce(mx[:, i % 2, :], s, AX.X, ALU.max).then_inc(av.sem, 1)
                    if b:
                        await_job(dve, bk, ("turn", b - 1, m, 3))
                    done(f"max{i}")
                    nc.vector.tensor_tensor(prob[:, m, r, :].rearrange("p (a k) -> p a k", a=8), s,
                                            mx[:, i % 2, :].unsqueeze(2).broadcast_to([P, 8, LC]), ALU.subtract
                                            ).then_inc(read_sem(j), 1)
                    if i:
                        normaliser(i - 1)
                normaliser(len(tiles) - 1)
                for b in R4:
                    for m in range(KD):
                        j = ("proj", b, m)
                        await_job(dve, bk, j)
                        nc.vector.scalar_tensor_tensor(X[b][m], abank(j), bproj[:, m:m + 1], X[b][m],
                                                       ALU.add, ALU.add).then_inc(read_sem(j), 1)
                for b in R4:
                    centre("mean3", b, "den")
                done(f"dsq{SLOTS - 1}")
                for b in R4:
                    scaled(b, ln3_w, "r3")
                for b in R4:
                    for r in range(4):
                        j = ("down", b, r)
                        dve.wait_ge(stored[r % 2], bk * 128 + (b * 2 + r // 2) * 16 + 16)
                        await_job(dve, bk, j)
                        nc.vector.tensor_copy(otile[:, r % 2, :], abank(j)[:, 0:D]).then_inc(read_sem(j), 1)

            dve.wait_ge(cst_loaded, 80)
            nc.vector.tensor_copy(spread[:, :, :], spread_f32.rearrange("p (j m) -> p j m", j=QUAD))
            dve.wait_ge(cst_exp, 1)
            nc.vector.tensor_scalar(negA[:, :, :], negA[:, :, :], -1.0, None, ALU.mult).then_inc(cst_neg, 1)
            dve.wait_ge(cst_neg, 1)
            for s in steps + [av, asc, apl]:
                nc.vector.sem_inc(s.sem, s.credit)
            for s in job_read + aread + [zw_free, ow_free]:
                nc.vector.sem_inc(s, 1)
            for s in list(stacked.values()) + stored:
                nc.vector.sem_inc(s, 16)
            nc.vector.sem_inc(cst_ready, 1)

            def head_and_pad(bk):
                head(bk)
                nc.vector.memset(xpad[:, :, 0:TAPS - 1], 0.0).then_inc(pad_ready, 1)
                dve.wait_ge(pad_ready, bk + 1)

            walk(dve, prepare_first, body, finish, attend, head_and_pad)

        @block.gpsimd
        def _(pool):
            def product(n, k, odd, base, c_back):
                if k == 0:
                    for h in range(2):
                        pool.wait_ge(job_read[h], base + (1 - c_back))
                pool.wait_ge(state.sem, state.before(n, 2 * k + 2))
                a = 2 * k % PRING
                nc.gpsimd.tensor_tensor(ring[:, a:a + 2, :], ring[:, a:a + 2, :],
                                        Crep[:, odd, :].unsqueeze(1).broadcast_to([P, 2, T]), ALU.mult
                                        ).then_inc(prod.sem, 1)

            def remainder(m, hc, k):
                pool.wait_ge(sdt[hc].sem, sdt[hc].upto(m, "hi_" + k))
                v = dt if k == "d" else lg
                if k == "d":
                    pool.wait_ge(vdt[hc].sem, vdt[hc].upto(m, "dtx"))
                nc.gpsimd.tensor_tensor(v, v, part["hi_" + k], ALU.subtract).then_inc(pdt[hc].sem, 1)

            def last_part(m, hc, k):
                pool.wait_ge(sdt[hc].sem, sdt[hc].upto(m, "mid_" + k))
                v = dt if k == "d" else lg
                nc.gpsimd.tensor_tensor(part["lo_" + k], v, part["mid_" + k], ALU.subtract
                                        ).then_inc(pdt[hc].sem, 1)

            POOL_AT = [(22, 23, 25, 26), (6, 7, 9, 10)]

            def dt_step(m, hc, name):
                (remainder if name[:2] == "r_" else last_part)(m, hc, name[-1])

            def body(order, base, n, odd):
                prep, first = "ms" in order, "out0" not in order
                for k in range(G // 2):
                    product(n, k, odd, base, (B_BACK_FIRST if first else B_BACK) - 1)
                    for name, at1, at0 in zip(POOL_DT, POOL_AT[1], POOL_AT[0]):
                        if at1 == k:
                            dt_step(n, 1, name)
                        if at0 == k and prep:
                            dt_step(n + 1, 0, name)

            def prepare_first(base, m):
                for name in POOL_DT:
                    dt_step(m, 0, name)

            def attend(bk):
                for i, (b, m, r) in enumerate(tiles):
                    pool.wait_ge(av.sem, av.upto(bk, f"rec{i}"))
                    v = prob[:, m, r, :].rearrange("p (a k) -> p a k", a=8)
                    nc.gpsimd.tensor_tensor(v, v, rden[:, i % 2, :].unsqueeze(2).broadcast_to([P, 8, LC]),
                                            ALU.mult).then_inc(apl.sem, 1)

            pool.wait_ge(cst_ready, 1)
            walk(pool, prepare_first, body, lambda base, nl: None, attend, lambda bk: None)

        @block.sync
        def _(sp):
            def split_rows(dst, src):
                yield dst[:, 0, :], src[0:P, :]
                yield dst[0:DC - P, 1, :], src[P:DC, :]

            for dst, src in ((csts[:, :], cst), (spread_f32, cst_spread), (avecs[:, :], avec), (negA[:, :, :], a_log), (Dall[:, :, :], d_par)):
                sp.dma_start(dst, src).then_inc(cst_loaded, 16)
            sp.wait_ge(cst_ready, 1)

            def stack(m, hc):
                for name, made in (("hi_d", sdt), ("hi_x", sdt), ("mid_d", sdt), ("mid_x", sdt),
                                   ("lo_d", pdt), ("lo_x", pdt)):
                    sp.wait_ge(made[hc].sem, made[hc].upto(m, name))
                    k, i = name[-1], ("hi", "mid", "lo").index(name[:-2])
                    for qq in range(QUAD):
                        sp.dma_start(st[k][32 * i:32 * i + 32, hc, qq:8:QUAD, :],
                                     part[name][32 * qq:32 * qq + 32, :, :]).then_inc(stacked[k, hc], 16)

            def row(v, lay):
                if isinstance(lay, int):
                    return v[lay].rearrange("(k p) m -> p k m", p=P)
                return v[bass.ds(lay, 1), :, :].rearrange("a (k p) m -> p (a k) m", p=P)

            def flat(v, lay):
                return v[lay] if isinstance(lay, int) else v[bass.ds(lay, 1), :, :].rearrange("a p m -> p (a m)")

            def early(done, lay):
                sp.dma_start(lv[:, 0:NP - KI], flat(w_early, lay)[:, 0:NP - KI]).then_inc(early_loaded, 16)
                sp.dma_start(ipx, row(ip_x, lay)).then_inc(early_loaded, 16)
                sp.wait_ge(early_loaded, done * 32 + 32)
                sp.sem_inc(early_ready, SLOTS)

            def late(done, lay):
                sp.dma_start(lv[:, NP - KI:NP], flat(w_early, lay)[:, NP - KI:NP]).then_inc(late_loaded, 16)
                sp.dma_start(xpw, row(xp_w, lay)).then_inc(late_loaded, 16)
                sp.dma_start(dtw[0:DR, :], flat(dt_w, lay)).then_inc(late_loaded, 16)
                sp.wait_ge(late_loaded, done * 48 + 48)
                sp.sem_inc(late_ready, SLOTS)

            def a_layer(lay, m0, done):
                mine = L - 1 if lay is None else lay
                stack(m0, 0)
                sp.wait_ge(zw_free, m0 + 1)
                sp.dma_start(ipz, row(ip_z, mine)).then_inc(z_loaded, 16)
                sp.wait_ge(z_loaded, done * 16 + 16)
                sp.sem_inc(zw_ready, SLOTS)
                stack(m0, 1)
                sp.wait_ge(ow_free, m0 + 1)
                sp.dma_start(opw, row(op_w, mine)).then_inc(o_loaded, 16)
                sp.wait_ge(o_loaded, done * 16 + 16)
                sp.sem_inc(ow_ready, SLOTS)
                for b in (1, 2):
                    for hc in range(2):
                        stack(m0 + b, hc)
                if lay is not None:
                    sp.wait_ge(vprep.sem, vprep.upto(m0 + 3, "silu3"))
                    early(done + 1, lay + 1)
                stack(m0 + 3, 0)
                if lay is not None:
                    sp.wait_ge(sdt[1].sem, sdt[1].upto(m0 + 3, "exp"))
                    late(done + 1, lay + 1)
                stack(m0 + 3, 1)

            with sp.Fori(0, BLOCKS) as bk:
                for i in range(2):
                    sp.wait_ge(stored[i], bk * 128 + 16)
                for b in range(SLOTS):
                    sp.dma_start(hT[:, b, :, LC:T],
                                 xT[bass.ds(bk * SLOTS + b, 1), :, :].rearrange("a (k p) t -> p (a k) t", p=P)
                                 ).then_inc(h_loaded, 16)
                mine = ctxT[:, bass.ds(bk * (SLOTS * LC), SLOTS * LC)]
                for dst, src in [*split_rows(ctxs, mine), *split_rows(pw1, pre_w1)]:
                    sp.dma_start(dst, src).then_inc(head_loaded, 16)
                sp.dma_start(pw2, pre_w2.rearrange("(k p) m -> p k m", p=P)).then_inc(head_loaded, 16)
                sp.wait_ge(pad_ready, bk + 1)
                early(bk * L, 0)
                late(bk * L, 0)
                with sp.Fori(0, L - 1) as lay:
                    a_layer(lay, bk * STEPS + lay * SLOTS, bk * L + lay)
                a_layer(None, bk * STEPS + (L - 1) * SLOTS, bk * L + (L - 1))
                sp.wait_ge(block_scanned, bk + 1)
                for dst, src in [(acst, cst_attention), *split_rows(ctxs, mine)]:
                    sp.dma_start(dst, src).then_inc(ctx_loaded, 16)
                for dst, src in [*split_rows(wk_s, wk), *split_rows(wv_s, wv)]:
                    sp.dma_start(dst, src).then_inc(aw_loaded, 16)
                for dst, src in ((wq_s, wq), (wp_s, wp), (w1_s, w1), (w2_s, w2)):
                    sp.dma_start(dst, src.rearrange("(k p) m -> p k m", p=P)).then_inc(aw_loaded, 16)
                sp.dma_start(b2_s[0:1, :], b2).then_inc(aw_loaded, 16)
                for b in range(SLOTS):
                    for r in range(4):
                        await_read(sp, bk, ("down", b, r))
                        sp.dma_start(out[bass.ds(bk * SLOTS + b, 1), r * P:(r + 1) * P, :]
                                     .rearrange("a t d -> t (a d)"), otile[:, r % 2, :]).then_inc(stored[r % 2], 16)
            for i in range(2):
                sp.wait_ge(stored[i], BLOCKS * 128 + 16)


def _inputs(x, ctx_768, **w):
    import numpy as np

    def a(name):
        return np.asarray(w[name])

    def f(v):
        return np.ascontiguousarray(v)

    def cols(v, n=P):
        return np.moveaxis(v.reshape(-1, n, *v.shape[1:]), 1, 0).reshape(n, -1)

    L0, L1 = "L0_xattn_", "L1_xattn_"
    early = [np.concatenate([cols(a(L0 + "norm_w")[i]), cols(a(L0 + "conv_w")[i]), cols(a(L0 + "conv_b")[i]),
                             cols(a(L0 + "dt_proj_b")[i])], 1) for i in range(L)]
    p = np.arange(P)
    cst = np.zeros((P, 512), np.float32)
    cst_spread = np.zeros((P, QUAD * P), np.float32)
    cst_attention = np.zeros((P, 424), np.float32)
    for j in range(QUAD):
        cst_spread[0:96, j * P:(j + 1) * P] = (p[:96, None] % 32) == CH * j + p[None, :] // DS
        cst[:, 32 * j:32 * (j + 1)] = p[:32][None, :] == CH * j + p[:, None] // DS
    cst[0:XP, 128:256] = p[:XP, None] == DR + p[None, :] % DS
    cst[0:XP, 256:384] = p[:XP, None] == DR + DS + p[None, :] % DS
    cst[:, 384:512] = 1.0 / D
    cst_attention[:, 0:128] = p[:, None] == p[None, :]
    cst_attention[:, 128:256] = 1.0
    cst_attention[:, 256:384] = 1.0 / DC
    cst_attention[:, 384:392] = p[:8][None, :] == p[:, None] // HD
    cst_attention[:, 392:424] = p[:32][None, :] // HD == p[:, None] // LC
    av = np.zeros((P, 32), np.float32)
    for i, name in enumerate(("ln1_w", "ln1_b", "ln3_w", "ln3_b", "bproj")):
        av[:, 2 * i:2 * i + 2] = cols(a(L1 + name))
    av[:, 10:12] = cols(a(L0 + "final_norm_w"))
    av[:, 12:20] = cols(a(L1 + "b1"))
    for i, name in ((20, "ln2_w"), (22, "ln2_b")):
        av[:, i] = a(L1 + name)[0:P]
        av[0:DC - P, i + 1] = a(L1 + name)[P:]
    ipT = a(L0 + "in_proj_w").transpose(0, 2, 1)
    return {
        "xT": f(np.asarray(x).transpose(0, 2, 1)),
        "ctxT": f(np.asarray(ctx_768).transpose(2, 0, 1).reshape(DC, B * LC)),
        "w_early": f(np.stack(early)),
        "ip_x": f(ipT[:, :, 0:DI]), "ip_z": f(ipT[:, :, DI:]),
        "xp_w": f(a(L0 + "x_proj_w").transpose(0, 2, 1)),
        "dt_w": f(a(L0 + "dt_proj_w").transpose(0, 2, 1)),
        "op_w": f(a(L0 + "out_proj_w").transpose(0, 2, 1)),
        "a_log": f(a(L0 + "A_log").reshape(L, G, P).transpose(2, 0, 1)),
        "d_par": f(a(L0 + "D_param").reshape(L, KI, P).transpose(2, 0, 1)),
        "pre_w1": f(a(L0 + "pre_w1")), "pre_w2": f(a(L0 + "pre_w2")),
        "cst": cst, "cst_spread": cst_spread, "cst_attention": cst_attention, "avec": av,
        "wq": f(a(L1 + "Wq")), "wk": f(a(L1 + "Wkv")[:, 0:D]), "wv": f(a(L1 + "Wkv")[:, D:]),
        "wp": f(a(L1 + "Wproj")), "w1": f(a(L1 + "W1")), "w2": f(a(L1 + "W2")),
        "b2": f(a(L1 + "b2").reshape(1, D)),
    }


def kernel(**inputs):
    import concourse.bacc as _bacc
    from concourse.bass_utils import run_bass_kernel_spmd as _run

    nc = _bacc.Bacc("TRN2", target_bir_lowering=False, num_devices=1)
    arrays = _inputs(**inputs)
    aps = {k: nc.dram_tensor(k, v.shape, F32, kind="ExternalInput").ap() for k, v in arrays.items()}
    aps["out"] = nc.dram_tensor("out", (B, S, D), F32, kind="ExternalOutput").ap()
    program(nc, **aps)
    r = _run(nc, [arrays], core_ids=[0])
    return r.results[0]["out"]
```
